# Optimizing a Trainium2 kernel written in Bass

```python
import numpy as np
import jax
import jax.numpy as jnp

def _softmax(x, axis=-1):
    return jax.nn.softmax(x, axis=axis)

def _gelu(x):
    return jax.nn.gelu(x, approximate=True)

def _silu(x):
    return jax.nn.silu(x)

def _sigmoid(x):
    return jax.nn.sigmoid(x)

def _layernorm(x, axis=-1, eps=1e-05):
    m = jnp.mean(x, axis=axis, keepdims=True)
    v = jnp.var(x, axis=axis, keepdims=True)
    return (x - m) / jnp.sqrt(v + eps)

def _scatter_add(tgt, idx, src, axis=0):
    return tgt.at[idx].add(src)

def _segment_sum(src, seg, n):
    return jax.ops.segment_sum(src, seg, n)
kernel_name = 'mk_seq_preln_d1_jaxref_r8_25745a'

def setup_inputs(seed: int=0):
    np.random.seed(seed)
    _w = jnp.asarray

    def _L0_attn_setup():
        import jax, jax.numpy as jnp
        import numpy as np
        EMBED = 128
        HEADS = 16
        HEAD_DIM = EMBED // HEADS
        NUM_BUCKETS = 32
        MAX_DISTANCE = 128
        B, L = (4, 256)

        def relative_position_bucket(relative_position, num_buckets=NUM_BUCKETS, max_distance=MAX_DISTANCE):
            n = -relative_position
            max_exact = num_buckets // 2
            is_small = n < max_exact
            nf = jnp.maximum(n, 1).astype(jnp.float32)
            val_if_large = max_exact + (jnp.log(nf / max_exact) / np.log(max_distance / max_exact) * (num_buckets - max_exact)).astype(jnp.int32)
            val_if_large = jnp.minimum(val_if_large, num_buckets - 1)
            ret = jnp.where(is_small, n, val_if_large)
            return jnp.maximum(ret, 0)
        key = jax.random.key(seed)
        ks = jax.random.split(key, 11)
        s = 0.02
        return {'x': jax.random.normal(ks[0], (B, L, EMBED), dtype=jnp.float32), 'wq': jax.random.normal(ks[1], (EMBED, EMBED), dtype=jnp.float32) * s, 'bq': jnp.zeros((EMBED,), dtype=jnp.float32), 'wk': jax.random.normal(ks[2], (EMBED, EMBED), dtype=jnp.float32) * s, 'bk': jnp.zeros((EMBED,), dtype=jnp.float32), 'wv': jax.random.normal(ks[3], (EMBED, EMBED), dtype=jnp.float32) * s, 'bv': jnp.zeros((EMBED,), dtype=jnp.float32), 'wo': jax.random.normal(ks[4], (EMBED, EMBED), dtype=jnp.float32) * s, 'bo': jnp.zeros((EMBED,), dtype=jnp.float32), 'rel_bias': jax.random.normal(ks[5], (NUM_BUCKETS, HEADS), dtype=jnp.float32) * s}
    _L0_attn_in = _L0_attn_setup()

    def _L0_ffn_setup():
        import jax, jax.numpy as jnp
        import numpy as np
        DIM = 128

        def _reference_tuple_inner(x, W_r, W_k, W_v, mu_r, mu_k):
            B, T, C = x.shape
            x_prev = jnp.concatenate([jnp.zeros((B, 1, C), x.dtype), x[:, :-1, :]], axis=1)
            xr = mu_r * x + (1.0 - mu_r) * x_prev
            xk = mu_k * x + (1.0 - mu_k) * x_prev
            r = jax.nn.sigmoid(jnp.einsum('btc,dc->btd', xr, W_r))
            k = jnp.einsum('btc,dc->btd', xk, W_k)
            k_act = jnp.square(jax.nn.relu(k))
            out = r * jnp.einsum('btc,dc->btd', k_act, W_v)
            new_state = x[:, -1, :]
            return (out, new_state)
        key = jax.random.key(seed)
        ks = jax.random.split(key, 6)
        B, T, C = (8, 256, DIM)
        x = jax.random.normal(ks[0], (B, T, C), dtype=jnp.float32)
        s = 1.0 / np.sqrt(C)
        W_r = jax.random.uniform(ks[1], (C, C), jnp.float32, -s, s)
        W_k = jax.random.uniform(ks[2], (C, C), jnp.float32, -s, s)
        W_v = jax.random.uniform(ks[3], (C, C), jnp.float32, -s, s)
        mu_r = jax.random.uniform(ks[4], (C,), jnp.float32)
        mu_k = jax.random.uniform(ks[5], (C,), jnp.float32)
        return {'x': x, 'W_r': W_r, 'W_k': W_k, 'W_v': W_v, 'mu_r': mu_r, 'mu_k': mu_k}
    _L0_ffn_in = _L0_ffn_setup()
    _d = {'L0_attn_x': _L0_attn_in['x'], 'L0_attn_wq': _L0_attn_in['wq'], 'L0_attn_bq': _L0_attn_in['bq'], 'L0_attn_wk': _L0_attn_in['wk'], 'L0_attn_bk': _L0_attn_in['bk'], 'L0_attn_wv': _L0_attn_in['wv'], 'L0_attn_bv': _L0_attn_in['bv'], 'L0_attn_wo': _L0_attn_in['wo'], 'L0_attn_bo': _L0_attn_in['bo'], 'L0_attn_rel_bias': _L0_attn_in['rel_bias'], 'L0_ffn_W_r': _L0_ffn_in['W_r'], 'L0_ffn_W_k': _L0_ffn_in['W_k'], 'L0_ffn_W_v': _L0_ffn_in['W_v'], 'L0_ffn_mu_r': _L0_ffn_in['mu_r'], 'L0_ffn_mu_k': _L0_ffn_in['mu_k']}
    _x0 = _d['L0_attn_x']
    _d['L0_attn_x'] = jax.random.normal(jax.random.fold_in(jax.random.key(seed), 1), (8, 512, 128), dtype=_x0.dtype)
    del _x0
    return _d

def reference(L0_attn_x, L0_attn_wq, L0_attn_bq, L0_attn_wk, L0_attn_bk, L0_attn_wv, L0_attn_bv, L0_attn_wo, L0_attn_bo, L0_attn_rel_bias, L0_ffn_W_r, L0_ffn_W_k, L0_ffn_W_v, L0_ffn_mu_r, L0_ffn_mu_k):

    def _L0_attn_ref(x, wq, bq, wk, bk, wv, bv, wo, bo, rel_bias):
        import jax, jax.numpy as jnp
        import numpy as np
        EMBED = 128
        HEADS = 16
        HEAD_DIM = EMBED // HEADS
        NUM_BUCKETS = 32
        MAX_DISTANCE = 128
        B, L = (4, 256)

        def relative_position_bucket(relative_position, num_buckets=NUM_BUCKETS, max_distance=MAX_DISTANCE):
            n = -relative_position
            max_exact = num_buckets // 2
            is_small = n < max_exact
            nf = jnp.maximum(n, 1).astype(jnp.float32)
            val_if_large = max_exact + (jnp.log(nf / max_exact) / np.log(max_distance / max_exact) * (num_buckets - max_exact)).astype(jnp.int32)
            val_if_large = jnp.minimum(val_if_large, num_buckets - 1)
            ret = jnp.where(is_small, n, val_if_large)
            return jnp.maximum(ret, 0)
        Bx, Lx, C = x.shape

        def proj(w, b):
            y = jnp.einsum('blc,dc->bld', x, w) + b
            return y.reshape(Bx, Lx, HEADS, HEAD_DIM).transpose(0, 2, 1, 3)
        q = proj(wq, bq)
        k = proj(wk, bk)
        v = proj(wv, bv)
        scores = jnp.einsum('bhqd,bhkd->bhqk', q, k) / np.sqrt(HEAD_DIM)
        ctx = jnp.arange(Lx, dtype=jnp.int32)
        relative = ctx[None, :] - ctx[:, None]
        bucket_ids = relative_position_bucket(relative)
        bias = rel_bias[bucket_ids]
        bias = jnp.transpose(bias, (2, 0, 1))
        attn = jax.nn.softmax(scores + bias[None], axis=-1)
        out = jnp.einsum('bhqk,bhkd->bhqd', attn, v)
        out = out.transpose(0, 2, 1, 3).reshape(Bx, Lx, C)
        return jnp.einsum('blc,dc->bld', out, wo) + bo

    def _L0_ffn_ref(x, W_r, W_k, W_v, mu_r, mu_k):
        import jax, jax.numpy as jnp
        import numpy as np
        DIM = 128

        def _reference_tuple_inner(x, W_r, W_k, W_v, mu_r, mu_k):
            B, T, C = x.shape
            x_prev = jnp.concatenate([jnp.zeros((B, 1, C), x.dtype), x[:, :-1, :]], axis=1)
            xr = mu_r * x + (1.0 - mu_r) * x_prev
            xk = mu_k * x + (1.0 - mu_k) * x_prev
            r = jax.nn.sigmoid(jnp.einsum('btc,dc->btd', xr, W_r))
            k = jnp.einsum('btc,dc->btd', xk, W_k)
            k_act = jnp.square(jax.nn.relu(k))
            out = r * jnp.einsum('btc,dc->btd', k_act, W_v)
            new_state = x[:, -1, :]
            return (out, new_state)
        return _reference_tuple_inner(x, W_r, W_k, W_v, mu_r, mu_k)[0]
    x = L0_attn_x
    x = x + _L0_attn_ref(_layernorm(x, axis=-1), L0_attn_wq, L0_attn_bq, L0_attn_wk, L0_attn_bk, L0_attn_wv, L0_attn_bv, L0_attn_wo, L0_attn_bo, L0_attn_rel_bias)
    x = x + _L0_ffn_ref(_layernorm(x, axis=-1), L0_ffn_W_r, L0_ffn_W_k, L0_ffn_W_v, L0_ffn_mu_r, L0_ffn_mu_k)
    return x

_drawn_inputs = setup_inputs


def setup_inputs(seed=0):
    import zlib

    import numpy as np

    out = dict(_drawn_inputs(seed))
    spreads = {'L0_attn_bq': (0.0, 0.8),
     'L0_attn_bk': (0.0, 2.0),
     'L0_attn_bv': (0.0, 0.378),
     'L0_attn_bo': (0.0, 0.1)}
    factors = {'L0_attn_wq': 8.0,
     'L0_attn_wk': 8.0,
     'L0_attn_wv': 8.0,
     'L0_attn_rel_bias': 37.421,
     'L0_ffn_W_r': 3.19,
     'L0_ffn_mu_r': 6.325}
    for name, (base, spread) in spreads.items():
        noise = np.random.default_rng([zlib.crc32(name.encode()), seed]).standard_normal(out[name].shape)
        drawn = base * np.exp(spread * noise) if base else spread * noise
        out[name] = jnp.asarray(drawn.astype(out[name].dtype))
    for name, factor in factors.items():
        out[name] = (out[name] * factor).astype(out[name].dtype)
    return out
```

```python
import math
from contextlib import ExitStack

import concourse.bass as bass
from concourse import mybir

F32 = mybir.dt.float32
BF16 = mybir.dt.bfloat16
I32 = mybir.dt.int32
ALU = mybir.AluOpType
ACT = mybir.ActivationFunctionType
AX_X = mybir.AxisListType.X

P = 128
BATCH, LEN, DIM = 8, 512, 128
HEADS, HD = 16, 8
NB = LEN // P
GROUPS, GH = 4, 4
UNITS = BATCH * GROUPS
STEPS = 8
BUCKETS, MAX_DISTANCE = 32, 128
EPS = 1e-5
RSQRT_MAGIC = float(0x5F3759DF)
NEWTON_STEPS = 3
NORM_LINKS = 2 + 2 + 3 * NEWTON_STEPS

Q_PART = [0, 0, 0, 1, 1, 2]
K_PART = [0, 1, 2, 0, 1, 0]
SLOTS = len(Q_PART)
QK_ROWS = SLOTS * HD
MAX_PASS_ROWS = 96
CONST_ROW = 96
SHIFT_ROW = CONST_ROW + 3 * NB
EXP_PASS_ROWS = SHIFT_ROW + 2

LINE = 2 * LEN
BAND = 2 * P
BAND_LINE = BAND + P


def bucket_first(k):
    half = BUCKETS // 2
    if k < half:
        return k
    return math.ceil(half * (MAX_DISTANCE / half) ** ((k - half) / (BUCKETS - half)) - 1e-9)


def bucket_ranges(lowest, highest):
    firsts = [lowest] + [bucket_first(k) for k in range(1, BUCKETS)] + [highest + 1]
    for k in range(BUCKETS):
        a, b = max(firsts[k], lowest), min(firsts[k + 1] - 1, highest)
        if a <= b:
            yield k, a, b


P_V_STEPS = [1, 3, 4, 7]

PE_AT = dict(max0=0, norm1=2, q=3, k=5, max1=9, v=10, max2=17, wo=18, norm2=21, max3=24, fk=26, fr=28, fv=30)
ACT_AT = dict(max0=2, xn_t=3, q=4, k=5, q_mid=5, k_mid=8, max1=10, v=11, max2=18, z_t=23, max3=25, fk=27, fr=28)
DVE_AT = dict(stats1=0, moments1=1, rstd1=1, norm1=2, q_low=6, k_low=9, v=7, invert=13, norm_o=17, residual=19, moments2=20, rstd2=20, norm2=21, mix=26, gate=31)
POOL_AT = dict(q_less=1, k_less=5, x_res=15, z_step=23, square=27, y=31)


def wait(eng, sem, value):
    if not isinstance(value, int) or value > 0:
        eng.wait_ge(sem, value)


def attention_ffn_program(nc, x, weights, columns, bo_row, rel_bias_t, y):
    ctx = ExitStack()
    with ctx:
        def sb(name, shape, dt=F32):
            return ctx.enter_context(nc.sbuf_tensor(name, shape, dt))

        def psum(name, shape):
            return ctx.enter_context(nc.psum_tensor(name, shape, F32))

        def sem(name):
            return ctx.enter_context(nc.semaphore(name))

        bias_line_dram = nc.dram_tensor("bias_line_dram", (HEADS, LINE), BF16, kind="Internal").ap()
        band_line_dram = nc.dram_tensor("band_line_dram", (HEADS, BAND_LINE), F32, kind="Internal").ap()
        image = [nc.dram_tensor(f"{n}_image", (QK_ROWS, HEADS, LEN), BF16, kind="Internal").ap() for n in "qk"]
        sums_dram = nc.dram_tensor("sums_dram", (HEADS, LEN), F32, kind="Internal").ap()
        inverse_dram = nc.dram_tensor("inverse_dram", (HEADS, LEN), F32, kind="Internal").ap()

        w_sb = sb("w_sb", [P, 7, DIM])
        WQ, WK, WV, WO, FR, FK, FV = range(7)
        col_sb = sb("col_sb", [P, 5])
        bo_sb = sb("bo_sb", [1, DIM])
        ones_row = sb("ones_row", [1, P])
        ident = sb("ident", [P, P])
        bv_wide = sb("bv_wide", [P, P])
        qk_bias = sb("qk_bias", [P, 2])
        proj_bias = sb("proj_bias", [P, DIM])
        q_stack = sb("q_stack", [P, HEADS, LEN], BF16)
        k_stack = sb("k_stack", [P, HEADS, LEN], BF16)
        bias_tab = sb("bias_tab", [P, HEADS, 2 * LEN - P], BF16)
        band_w = sb("band_w", [P, HEADS, BAND])
        probs = [sb(f"probs{n}", [P, GH, NB * LEN]) for n in range(2)]
        v_sb = sb("v_sb", [P, NB, HEADS, 32])
        v_stage = sb("v_stage", [P, NB * DIM])
        maxes = [sb(f"maxes{n}", [P, GH * NB]) for n in range(2)]
        shift_f = sb("shift_f", [GH * NB, P])
        shift_parts = [sb(f"shift_parts{n}", [GH * NB, 2, P], BF16) for n in range(2)]
        x_in = sb("x_in", [P, NB, DIM])
        xn = sb("xn", [P, NB, DIM])
        xn_t = sb("xn_t", [P, LEN])
        qk_f = sb("qk_f", [P, 2, LEN])
        parts = sb("parts", [P, 2, 3, LEN], BF16)
        o_t = [sb(f"o_t{n}", [P, LEN]) for n in range(2)]
        numer = sb("numer", [P, LEN])
        inverse = sb("inverse", [P, LEN])
        sums = sb("sums", [P, HEADS * LEN // P])
        x_res = sb("x_res", [P, NB, DIM])
        x1 = sb("x1", [P, NB, DIM])
        zn = xn
        z_t = sb("z_t", [P, LEN + 1])
        z_step = sb("z_step", [P, LEN])
        z_k = sb("z_k", [P, LEN])
        z_r = sb("z_r", [P, LEN])
        k_relu = sb("k_relu", [P, LEN])
        k_act = sb("k_act", [P, LEN])
        gate = sb("gate", [P, NB, DIM])
        gated = sb("gated", [P, NB, DIM])
        y_sb = gated
        stats = [sb(f"stats{n}", [P, NB, 6]) for n in range(2)]
        moments = [sb(f"moments{n}", [P, NB, 2]) for n in range(2)]
        rstd = [sb(f"rstd{n}", [P, NB]) for n in range(2)]
        variance = [sb(f"variance{n}", [P, NB]) for n in range(2)]
        newton = [sb(f"newton{n}", [P, NB]) for n in range(2)]
        rb_sb = sb("rb_sb", [HEADS, BUCKETS])
        rb_c = sb("rb_c", [HEADS, BUCKETS])
        rb_lim = sb("rb_lim", [HEADS, 3])
        cv = sb("cv", [HEADS, 3])
        cv_parts = sb("cv_parts", [HEADS, 3, 3], BF16)
        bias_line = probs[0][0:HEADS, 0, 0:LINE // 2].bitcast(BF16)
        band_line = probs[0][0:HEADS, 1, 0:BAND_LINE]
        band_raw = probs[0][:, 2:4, :]
        const_rows = probs[1][0:HEADS, 0:3, 0:NB * LEN // 2].bitcast(BF16)

        ps_max = [psum(f"ps_max{n}", [P, LEN]) for n in range(2)]
        ps_exp = [psum(f"ps_exp{n}", [P, 2, LEN]) for n in range(2)]
        ps_out = psum("ps_out", [P, LEN])
        ps_misc = psum("ps_misc", [P, LEN])

        weights_loaded, rb_loaded = sem("weights_loaded"), sem("rb_loaded")
        setup_dve, setup_pool = sem("setup_dve"), sem("setup_pool")
        bv_wide_ready = sem("bv_wide_ready")
        lines_ready, lines_stored = sem("lines_ready"), sem("lines_stored")
        bias_loaded = [sem(f"bias_loaded{g}") for g in range(GROUPS)]
        band_loaded, band_ready = sem("band_loaded"), sem("band_ready")
        const_rows_ready, const_rows_loaded = sem("const_rows_ready"), sem("const_rows_loaded")
        stacks_zeroed, k_const_ready, ident_ready = sem("stacks_zeroed"), sem("k_const_ready"), sem("ident_ready")
        v_ones_ready, z_zero_ready = sem("v_ones_ready"), sem("z_zero_ready")
        centre_ready = sem("centre_ready")
        proj_bias_done, proj_bias_ready = sem("proj_bias_done"), sem("proj_bias_ready")
        qk_bias_ready, fv_halved = sem("qk_bias_ready"), sem("fv_halved")
        x_loaded, norm1_chain, xn_ready = sem("x_loaded"), sem("norm1_chain"), sem("xn_ready")
        xn_transposed, xn_t_ready = sem("xn_transposed"), sem("xn_t_ready")
        qk_projected, qk_copied = sem("qk_projected"), sem("qk_copied")
        qk_less_high, qk_mid_ready, qk_split = sem("qk_less_high"), sem("qk_mid_ready"), sem("qk_split")
        image_written = [sem("q_image_written"), sem("k_image_written")]
        stacks_loaded = [sem(f"stacks_loaded{g}") for g in range(GROUPS)]
        v_projected, v_staged, v_ready = sem("v_projected"), sem("v_staged"), sem("v_ready")
        max_scored, maxed = sem("max_scored"), sem("maxed")
        max_transposed, shift_copied, shift_split = sem("max_transposed"), sem("shift_copied"), sem("shift_split")
        shift_loaded = [sem(f"shift_loaded{n}") for n in range(2)]
        exp_scored, exped, banded = sem("exp_scored"), sem("exped"), sem("banded")
        pv_done, o_copied = sem("pv_done"), sem("o_copied")
        o_moved = [sem(f"o_moved{n}") for n in range(2)]
        sums_stored = [sem(f"sums_stored{n}") for n in range(2)]
        sums_loaded, inverted, inverse_stored = sem("sums_loaded"), sem("inverted"), sem("inverse_stored")
        inverse_loaded, o_normed = sem("inverse_loaded"), sem("o_normed")
        x_res_loaded, x_res_biased, attn_projected, x1_ready = (
            sem("x_res_loaded"), sem("x_res_biased"), sem("attn_projected"), sem("x1_ready"))
        norm2_chain, zn_ready, zn_transposed, z_t_ready = (
            sem("norm2_chain"), sem("zn_ready"), sem("zn_transposed"), sem("z_t_ready"))
        z_step_ready, z_mixed = sem("z_step_ready"), sem("z_mixed")
        fk_projected, k_relu_ready, k_act_ready = sem("fk_projected"), sem("k_relu_ready"), sem("k_act_ready")
        fr_projected, gate_ready, fv_projected, gated_ready = (
            sem("fr_projected"), sem("gate_ready"), sem("fv_projected"), sem("gated_ready"))
        y_ready, y_stored = sem("y_ready"), sem("y_stored")

        waits_apart = sem("waits_apart")

        def wait_apart(eng, sem_, value):
            if isinstance(value, int):
                wait(eng, sem_, value)
            else:
                eng.wait_ge(sem_, value)
                eng.sem_inc(waits_apart, 1)

        def turn(b, g):
            return 2 * b + g // 2

        block = ctx.enter_context(nc.Block())

        def run(eng, prologue, iteration, epilogue, alike=BATCH - 3):
            prologue()
            iteration(0, first=True)
            iteration(1)
            with eng.Fori(2, 2 + alike) as i:
                iteration(i)
            for i in range(2 + alike, BATCH):
                iteration(i, last=i == BATCH - 1)
            epilogue()


        @block.sync
        def _(sp):
            def load_x(b):
                wait_apart(sp, xn_ready, b)
                sp.dma_start(x_in[:, :, :], x[b]).then_inc(x_loaded, 16)

            def write_image(b, t):
                wait_apart(sp, qk_split, 2 * b + t + 1)
                for g in range(GROUPS):
                    wait_apart(sp, stacks_loaded[g], 32 * b)
                for s in range(SLOTS):
                    part = (Q_PART, K_PART)[t][s]
                    sp.dma_start(image[t][s * HD:(s + 1) * HD].rearrange("d h t -> h d t"),
                                 parts[:, t, part, :]).then_inc(image_written[t], 16)

            def load_stacks(b, g):
                u = 4 * b + g
                wait_apart(sp, image_written[0], 16 * SLOTS * (b + 1))
                wait_apart(sp, image_written[1], 16 * SLOTS * (b + 1))
                wait_apart(sp, exp_scored, STEPS * (u - GROUPS + 1))
                for stack, im in ((q_stack, image[0]), (k_stack, image[1])):
                    sp.dma_start(stack[0:QK_ROWS, 4 * g:4 * g + 4, :],
                                 im[:, 4 * g:4 * g + 4, :]).then_inc(stacks_loaded[g], 16)

            def load_shift(b, g):
                wait_apart(sp, shift_split, 4 * b + g + 1)
                for part in range(2):
                    sp.dma_start(q_stack[SHIFT_ROW + part:SHIFT_ROW + part + 1, 4 * g:4 * g + 4, :],
                                 shift_parts[g % 2][:, part, :]).then_inc(shift_loaded[g % 2], 16)

            def move_o(b, g):
                u = 4 * b + g
                wait_apart(sp, o_copied, u + 1)
                if g == 0:
                    wait_apart(sp, attn_projected, b)
                    wait_apart(sp, sums_loaded, 16 * b)
                for j in range(GH):
                    sp.dma_start(numer[32 * g + 8 * j:32 * g + 8 * j + 8, :],
                                 o_t[g % 2][32 * j:32 * j + HD, :]).then_inc(o_moved[g % 2], 16)
                sp.dma_start(sums_dram[4 * g:4 * g + 4, :],
                             o_t[g % 2][HD:P:32, :]).then_inc(sums_stored[g % 2], 16)

            def load_sums(b):
                for n in range(2):
                    wait_apart(sp, sums_stored[n], 32 * (b + 1))
                wait_apart(sp, inverse_stored, 16 * b)
                sp.dma_start(sums[:, :], sums_dram.rearrange("h (r c) -> (h r) c", c=HEADS * LEN // P)
                             ).then_inc(sums_loaded, 16)

            def spread_inverse(b):
                wait_apart(sp, inverted, b + 1)
                wait_apart(sp, inverse_loaded, 16 * b)
                sp.dma_start(inverse_dram.rearrange("h (r c) -> (h r) c", c=HEADS * LEN // P),
                             sums[:, :]).then_inc(inverse_stored, 16)
                wait_apart(sp, inverse_stored, 16 * (b + 1))
                wait_apart(sp, o_normed, b)
                sp.dma_start(inverse[:, :], bass.AP(inverse_dram.tensor, 0, [[LEN, HEADS], [0, HD], [1, LEN]])
                             ).then_inc(inverse_loaded, 16)

            def load_x_res(b):
                wait_apart(sp, x1_ready, b)
                sp.dma_start(x_res[:, :, :], x[b]).then_inc(x_res_loaded, 16)

            def store_y(b):
                wait_apart(sp, y_ready, b + 1)
                sp.dma_start(y[b], y_sb[:, :, :]).then_inc(y_stored, 16)

            def prologue():
                load_x(0)
                sp.dma_start(rb_sb[:, :], rel_bias_t).then_inc(rb_loaded, 16)
                sp.dma_start(w_sb[:, :, :], weights).then_inc(weights_loaded, 16)
                sp.dma_start(col_sb[:, :], columns).then_inc(weights_loaded, 16)
                sp.dma_start(bo_sb[:, :], bo_row).then_inc(weights_loaded, 16)
                sp.wait_ge(lines_ready, 2)
                sp.dma_start(bias_line_dram, bias_line).then_inc(lines_stored, 16)
                sp.dma_start(band_line_dram, band_line).then_inc(lines_stored, 16)
                sp.wait_ge(lines_stored, 32)
                sp.dma_start(bias_tab[:, 0:4, :], bass.AP(bias_line_dram.tensor, 0, [
                    [1, P], [LINE, GH], [1, 2 * LEN - P]])).then_inc(bias_loaded[0], 16)
                load_x(1)
                sp.dma_start(band_raw, bass.AP(band_line_dram.tensor, 0, [
                    [1, P], [BAND_LINE, HEADS], [1, BAND]])).then_inc(band_loaded, 16)
                sp.wait_ge(stacks_zeroed, 2)
                sp.wait_ge(const_rows_ready, 1)
                for r in range(3 * NB):
                    sp.dma_start(q_stack[CONST_ROW + r:CONST_ROW + r + 1, :, :],
                                 const_rows[:, r // NB, (r % NB) * LEN:(r % NB + 1) * LEN]
                                 ).then_inc(const_rows_loaded, 16)
                write_image(0, 0)
                write_image(0, 1)
                for g in range(GROUPS):
                    load_stacks(0, g)
                for g in range(1, GROUPS):
                    sp.dma_start(bias_tab[:, 4 * g:4 * g + 4, :], bass.AP(
                        bias_line_dram.tensor, 4 * g * LINE, [
                            [1, P], [LINE, GH], [1, 2 * LEN - P]])).then_inc(bias_loaded[g], 16)
                load_shift(0, 0)

            def iteration(i, first=False, last=False):
                if not first:
                    move_o(i - 1, 2)
                    load_stacks(i, 3)
                load_shift(i, 1)
                if not last:
                    write_image(i + 1, 0)
                if not first:
                    move_o(i - 1, 3)
                if not last:
                    write_image(i + 1, 1)
                if not first:
                    load_sums(i - 1)
                if not last:
                    load_stacks(i + 1, 0)
                load_shift(i, 2)
                if not first:
                    spread_inverse(i - 1)
                    load_x_res(i - 1)
                move_o(i, 0)
                if not last:
                    load_stacks(i + 1, 1)
                load_shift(i, 3)
                if not isinstance(i, int) or i + 2 < BATCH:
                    load_x(i + 2)
                move_o(i, 1)
                if not last:
                    load_stacks(i + 1, 2)
                    load_shift(i + 1, 0)
                if not first:
                    store_y(i - 1)

            def epilogue():
                move_o(BATCH - 1, 2)
                move_o(BATCH - 1, 3)
                load_sums(BATCH - 1)
                spread_inverse(BATCH - 1)
                load_x_res(BATCH - 1)
                store_y(BATCH - 1)
                sp.wait_ge(y_stored, 16 * BATCH)

            run(sp, prologue, iteration, epilogue, alike=BATCH - 4)

        @block.tensor
        def _(pe):
            def max_scores(u, h, qb, n):
                number = 16 * u + n
                wait(pe, maxed, number - 1)
                pe.matmul(ps_max[n % 2][:, :], q_stack[0:MAX_PASS_ROWS, h, qb * P:(qb + 1) * P],
                          k_stack[0:MAX_PASS_ROWS, h, :], start=True, stop=True).then_inc(max_scored, 1)

            def exp_scores(w, h, s):
                wait(pe, exped, STEPS * w + s - 1)
                for n in range(2):
                    kb = 2 * (s % 2) + n
                    mm = pe.matmul(ps_exp[s % 2][:, n, :], k_stack[0:EXP_PASS_ROWS, h, kb * P:(kb + 1) * P],
                                   q_stack[0:EXP_PASS_ROWS, h, :], start=True, stop=True)
                mm.then_inc(exp_scored, 1)

            def p_v(w, g, n, kb):
                if kb == 0:
                    wait(pe, banded, 4 * w + 4)
                    wait(pe, o_copied, w)
                for j in range(GH):
                    mm = pe.matmul(ps_out[32 * j:32 * j + 32, :], v_sb[:, kb, 4 * g + j, :],
                                   probs[n][:, j, kb * LEN:(kb + 1) * LEN], start=kb == 0, stop=kb == NB - 1)
                if kb == NB - 1:
                    mm.then_inc(pv_done, 1)

            def transpose_maxima(u, n):
                wait(pe, maxed, 16 * (u + 1))
                pe.matmul(ps_misc[0:GH * NB, 0:P], maxes[n][:, :], ident[:, :],
                          start=True, stop=True).then_inc(max_transposed, 1)

            def transposes(tile, ready, count, done):
                wait(pe, ready, count)
                for blk in range(NB):
                    mm = pe.transpose(ps_misc[:, blk * P:(blk + 1) * P], tile[:, blk, :], ident[:, :])
                mm.then_inc(done, 1)

            def channels_out(w, moving, done):
                pe.matmul(ps_misc[:, :], w_sb[:, w, :], moving, start=True, stop=True).then_inc(done, 1)

            def tokens_out(w, stationary, done):
                for blk in range(NB):
                    mm = pe.matmul(ps_misc[:, blk * DIM:(blk + 1) * DIM], stationary[:, blk * P:(blk + 1) * P],
                                   w_sb[:, w, :], start=True, stop=True)
                mm.then_inc(done, 1)

            def norm1_transposes(b):
                transposes(xn, xn_ready, b + 1, xn_transposed)

            def project_qk(b, t):
                if t == 0:
                    wait(pe, xn_t_ready, b + 1)
                else:
                    wait(pe, qk_copied, 2 * b + 1)
                channels_out((WQ, WK)[t], xn_t[:, :], qk_projected)

            def project_v(b):
                tokens_out(WV, xn_t, v_projected)

            def project_o(b):
                wait(pe, o_normed, b + 1)
                tokens_out(WO, numer, attn_projected)

            def norm2_transposes(b):
                wait(pe, x1_ready, b + 1)
                transposes(zn, zn_ready, b + 1, zn_transposed)

            def ffn_k(b):
                wait(pe, z_mixed, b + 1)
                channels_out(FK, z_k[:, :], fk_projected)

            def ffn_r(b):
                wait(pe, k_relu_ready, b + 1)
                tokens_out(FR, z_r, fr_projected)

            def ffn_v(b):
                wait(pe, gate_ready, b + 1)
                wait(pe, k_act_ready, b + 1)
                tokens_out(FV, k_act, fv_projected)

            def prologue():
                pe.wait_ge(weights_loaded, 48)
                pe.wait_ge(bv_wide_ready, 2)
                pe.wait_ge(ident_ready, 1)
                pe.wait_ge(fv_halved, 1)
                pe.matmul(ps_misc[:, 0:DIM], bv_wide[:, :], w_sb[:, WO, :], start=True, stop=False)
                pe.matmul(ps_misc[:, 0:DIM], ones_row[:, :], bo_sb[:, :],
                          start=False, stop=True).then_inc(proj_bias_done, 1)
                pe.wait_ge(proj_bias_ready, 1)
                norm1_transposes(0)
                project_qk(0, 0)
                project_qk(0, 1)
                pe.wait_ge(qk_copied, 2)
                project_v(0)
                pe.wait_ge(k_const_ready, 1)
                for u in range(2):
                    pe.wait_ge(stacks_loaded[u], 32)
                    for n in range(4 * GH):
                        max_scores(u, 4 * u + n // NB, n % NB, n)
                    if u == 0:
                        pe.wait_ge(v_staged, 1)
                        transpose_maxima(0, 0)

            def iteration(i, first=False, last=False):
                for g in range(GROUPS):
                    w = 4 * i + g
                    wait(pe, shift_loaded[g % 2], 32 * (turn(i, g) + 1))
                    maxima = not last or g < 2
                    if maxima:
                        wait(pe, stacks_loaded[(g + 2) % 4], 32 * (i + 1 + g // 2))
                    if first and g == 0:
                        pe.wait_ge(const_rows_loaded, 16 * 3 * NB)
                    for s in range(STEPS):
                        at = STEPS * g + s
                        exp_scores(w, 4 * g + s // 2, s)
                        if maxima:
                            for n in (2 * s, 2 * s + 1):
                                max_scores(w + 2, 4 * ((g + 2) % 4) + n // NB, n % NB, n)
                        if s in P_V_STEPS and not (first and g == 0):
                            if g == 1 and s == P_V_STEPS[0]:
                                wait(pe, v_ready, i + 1)
                            p_v(w - 1, (g - 1) % 4, (g - 1) % 2, P_V_STEPS.index(s))
                        if at == PE_AT[f"max{g}"] and not (last and g == 3):
                            if g == 0 and not first:
                                wait(pe, gated_ready, i - 1)
                            elif g == 1 and not last:
                                wait(pe, qk_copied, 2 * i + 4)
                            elif g == 3 and not first:
                                wait(pe, z_t_ready, i)
                            elif g == 2 and not last:
                                wait(pe, v_staged, i + 2)
                            wait(pe, shift_copied, w + 1)
                            transpose_maxima(w + 1, (g + 1) % 2)
                        if not last:
                            if at == PE_AT["norm1"]:
                                wait(pe, shift_copied, w + 2)
                                norm1_transposes(i + 1)
                            if at == PE_AT["q"]:
                                project_qk(i + 1, 0)
                            if at == PE_AT["k"]:
                                project_qk(i + 1, 1)
                            if at == PE_AT["v"]:
                                wait(pe, shift_copied, w + 2)
                                project_v(i + 1)
                        if not first:
                            if at == PE_AT["wo"]:
                                wait(pe, shift_copied, w + 2)
                                project_o(i - 1)
                            if at == PE_AT["norm2"]:
                                norm2_transposes(i - 1)
                            if at == PE_AT["fk"]:
                                if last:
                                    wait(pe, z_t_ready, i)
                                else:
                                    wait(pe, shift_copied, w + 2)
                                ffn_k(i - 1)
                            if at == PE_AT["fr"]:
                                ffn_r(i - 1)
                            if at == PE_AT["fv"]:
                                ffn_v(i - 1)

            def epilogue():
                for kb in range(NB):
                    p_v(UNITS - 1, GROUPS - 1, 1, kb)
                b = BATCH - 1
                pe.wait_ge(gated_ready, b)
                project_o(b)
                norm2_transposes(b)
                pe.wait_ge(z_t_ready, b + 1)
                ffn_k(b)
                ffn_r(b)
                ffn_v(b)

            run(pe, prologue, iteration, epilogue)

        @block.scalar
        def _(act):
            def exponentials(w, n, s):
                if s == 0:
                    wait(act, pv_done, w - 1)
                wait(act, exp_scored, STEPS * w + s + 1)
                nc.scalar.activation(
                    probs[n][:, s // 2, (s % 2) * 2 * LEN:(s % 2 + 1) * 2 * LEN],
                    ps_exp[s % 2][:, :, :].rearrange("p a b -> p (a b)"), ACT.Exp).then_inc(exped, 1)

            def exp_band():
                act.wait_ge(band_loaded, 16)
                raw = bass.AP(probs[0], 2 * NB * LEN + BAND - 1, [[GH * NB * LEN, P], [BAND, HEADS], [-1, BAND]])
                nc.scalar.activation(band_w[:, :, :], raw, ACT.Exp).then_inc(band_ready, 1)

            def copy_o(b, g):
                n = g % 2
                wait(act, o_moved[n], 64 * turn(b, g))
                wait(act, sums_stored[n], 16 * turn(b, g))
                wait(act, pv_done, 4 * b + g + 1)
                nc.scalar.activation(o_t[n][:, :], ps_out[:, :], ACT.Copy).then_inc(o_copied, 1)

            def copy_shift(b, g):
                u, n = 4 * b + g, g % 2
                wait(act, shift_loaded[n], 32 * turn(b, g))
                wait(act, max_transposed, u + 1)
                nc.scalar.activation(shift_parts[n][:, 0, :], ps_misc[0:GH * NB, 0:P], ACT.Copy, scale=-1.0)
                wait(act, shift_split, u)
                nc.scalar.activation(shift_f[:, :], ps_misc[0:GH * NB, 0:P], ACT.Copy,
                                     scale=-1.0).then_inc(shift_copied, 1)

            def copy_xn_t(b):
                wait(act, xn_transposed, b + 1)
                nc.scalar.activation(xn_t[:, :], ps_misc[:, :], ACT.Copy).then_inc(xn_t_ready, 1)

            def copy_qk(b, t):
                wait(act, image_written[t], 16 * SLOTS * b)
                wait(act, qk_split, 2 * b + t - 1)
                wait(act, qk_projected, 2 * b + t + 1)
                scale = (float(HD) ** -0.5, 1.0)[t]
                nc.scalar.activation(qk_f[:, t, :], ps_misc[:, :], ACT.Identity,
                                     bias=qk_bias[:, t:t + 1], scale=scale)
                nc.scalar.activation(parts[:, t, 0, :], ps_misc[:, :], ACT.Identity,
                                     bias=qk_bias[:, t:t + 1], scale=scale).then_inc(qk_copied, 1)

            def mid_part(b, t):
                wait(act, qk_less_high, 2 * b + t + 1)
                nc.scalar.activation(parts[:, t, 1, :], qk_f[:, t, :], ACT.Copy).then_inc(qk_mid_ready, 1)

            def stage_v(b):
                wait(act, v_ready, b)
                wait(act, v_projected, b + 1)
                nc.scalar.activation(v_stage[:, :], ps_misc[:, :], ACT.Copy).then_inc(v_staged, 1)

            def copy_z_t(b):
                wait(act, z_mixed, b)
                wait(act, zn_transposed, b + 1)
                nc.scalar.activation(z_t[:, 1:LEN + 1], ps_misc[:, :], ACT.Copy).then_inc(z_t_ready, 1)

            def relu_k(b):
                wait(act, k_act_ready, b)
                wait(act, fk_projected, b + 1)
                nc.scalar.activation(k_relu[:, :], ps_misc[:, :], ACT.Relu).then_inc(k_relu_ready, 1)

            def gate_tanh(b):
                wait(act, gated_ready, b)
                wait(act, fr_projected, b + 1)
                nc.scalar.activation(gate[:, :, :].rearrange("p a b -> p (a b)"), ps_misc[:, :], ACT.Tanh,
                                     scale=0.5).then_inc(gate_ready, 1)

            def prologue():
                act.wait_ge(proj_bias_done, 1)
                nc.scalar.activation(proj_bias[:, :], ps_misc[:, 0:DIM], ACT.Copy).then_inc(proj_bias_ready, 1)
                copy_xn_t(0)
                act.wait_ge(qk_bias_ready, 1)
                for t in range(2):
                    copy_qk(0, t)
                for t in range(2):
                    mid_part(0, t)
                stage_v(0)
                exp_band()
                copy_shift(0, 0)
                act.wait_ge(const_rows_loaded, 16 * 3 * NB)

            def iteration(i, first=False, last=False):
                for g in range(GROUPS):
                    w = 4 * i + g
                    for s in range(STEPS):
                        at = STEPS * g + s
                        exponentials(w, g % 2, s)
                        if s == 0 and not (first and g < 2):
                            copy_o(i - 1 if g < 2 else i, (g + 2) % 4)
                        if at == ACT_AT[f"max{g}"] and not (last and g == 3):
                            copy_shift(i + (g + 1) // 4, (g + 1) % 4)
                        if not last:
                            if at == ACT_AT["xn_t"]:
                                copy_xn_t(i + 1)
                            if at == ACT_AT["q"]:
                                copy_qk(i + 1, 0)
                            if at == ACT_AT["k"]:
                                copy_qk(i + 1, 1)
                            if at == ACT_AT["q_mid"]:
                                mid_part(i + 1, 0)
                            if at == ACT_AT["k_mid"]:
                                mid_part(i + 1, 1)
                            if at == ACT_AT["v"]:
                                stage_v(i + 1)
                        if not first:
                            if at == ACT_AT["z_t"]:
                                copy_z_t(i - 1)
                            if at == ACT_AT["fk"]:
                                relu_k(i - 1)
                            if at == ACT_AT["fr"]:
                                gate_tanh(i - 1)

            def epilogue():
                copy_o(BATCH - 1, 2)
                copy_o(BATCH - 1, 3)
                b = BATCH - 1
                copy_z_t(b)
                relu_k(b)
                gate_tanh(b)

            run(act, prologue, iteration, epilogue)

        @block.vector
        def _(dve):
            chain = [0]

            def link(ins):
                chain[0] += 1
                ins.then_inc(setup_dve, 1)
                dve.wait_ge(setup_dve, chain[0])

            def maximum(u, h, qb, n):
                if n == 0:
                    wait(dve, max_transposed, u - 1)
                wait_apart(dve, max_scored, 16 * u + n + 1)
                window = bass.AP(bias_tab, h * (2 * LEN - P) + LEN - 1 + qb * P,
                                 [[HEADS * (2 * LEN - P), P], [-1, LEN]])
                nc.vector.tensor_tensor_reduce(
                    ps_max[n % 2][:, :], ps_max[n % 2][:, :], window, 1.0, -3.0e38,
                    ALU.add, ALU.max, maxes[(h // GH) % 2][:, n:n + 1]).then_inc(maxed, 1)

            def norm_stats(k, tile, done):
                for blk in range(NB):
                    ins = nc.vector.bn_stats(stats[k][:, blk, :], tile[:, blk, :])
                ins.then_inc(done, 1)

            def norm_moments(k, b, done):
                wait_apart(dve, done, NORM_LINKS * b + 1)
                for blk in range(NB):
                    ins = nc.vector.bn_aggr(moments[k][:, blk, :], stats[k][:, blk, :])
                ins.then_inc(done, 1)

            def norm_rstd(k, b, done):
                links = [NORM_LINKS * b + 1]

                def next_link():
                    links[0] = links[0] + 1
                    wait(dve, done, links[0])

                var, r, t = variance[k], rstd[k], newton[k]
                next_link()
                nc.vector.tensor_scalar(var[:, :], moments[k][:, :, 1], EPS, None, ALU.add).then_inc(done, 1)
                next_link()
                nc.vector.tensor_scalar(r[:, :].bitcast(I32), var[:, :].bitcast(I32), -0.5, RSQRT_MAGIC,
                                        ALU.mult, ALU.add).then_inc(done, 1)
                for _ in range(NEWTON_STEPS):
                    next_link()
                    nc.vector.scalar_tensor_tensor(out=t[:, :], in0=r[:, :], scalar=-0.5, in1=r[:, :],
                                                   op0=ALU.mult, op1=ALU.mult).then_inc(done, 1)
                    next_link()
                    nc.vector.tensor_tensor(t[:, :], t[:, :], var[:, :], ALU.mult).then_inc(done, 1)
                    next_link()
                    nc.vector.scalar_tensor_tensor(out=r[:, :], in0=t[:, :], scalar=1.5, in1=r[:, :],
                                                   op0=ALU.add, op1=ALU.mult).then_inc(done, 1)

            def norm_apply(k, b, tile, out, done, ready):
                wait(dve, done, NORM_LINKS * (b + 1))
                for blk in range(NB):
                    ins = nc.vector.tensor_scalar(out[:, blk, :], tile[:, blk, :], moments[k][:, blk, 0:1],
                                                  rstd[k][:, blk:blk + 1], ALU.subtract, ALU.mult)
                ins.then_inc(ready, 1)

            def norm1_stats(b):
                wait_apart(dve, x_loaded, 16 * (b + 1))
                norm_stats(0, x_in, norm1_chain)

            def norm1_apply(b):
                wait(dve, zn_transposed, b - 2)
                wait(dve, xn_transposed, b)
                norm_apply(0, b, x_in, xn, norm1_chain, xn_ready)

            def low_part(b, t):
                wait(dve, qk_mid_ready, 2 * b + t + 1)
                nc.vector.tensor_tensor(parts[:, t, 2, :], qk_f[:, t, :], parts[:, t, 1, :],
                                        ALU.subtract).then_inc(qk_split, 1)

            def place_v(b):
                wait(dve, v_staged, b + 1)
                wait(dve, pv_done, 4 * b)
                nc.vector.tensor_copy(v_sb[:, :, :, 0:HD], v_stage[:, :].rearrange(
                    "p (n h d) -> p n h d", n=NB, h=HEADS)).then_inc(v_ready, 1)

            def invert_sums(b):
                wait(dve, sums_loaded, 16 * (b + 1))
                nc.vector.reciprocal(sums[:, :], sums[:, :]).then_inc(inverted, 1)

            def norm_o(b):
                for n in range(2):
                    wait(dve, o_moved[n], 128 * (b + 1))
                wait(dve, inverse_loaded, 16 * (b + 1))
                nc.vector.tensor_tensor(numer[:, :], numer[:, :], inverse[:, :], ALU.mult).then_inc(o_normed, 1)

            def add_residual(b):
                wait(dve, y_ready, b)
                wait(dve, x_res_biased, b + 1)
                wait(dve, attn_projected, b + 1)
                nc.vector.tensor_tensor(x1[:, :, :], ps_misc[:, :].rearrange("p (a b) -> p a b", a=NB),
                                        x_res[:, :, :], ALU.add).then_inc(x1_ready, 1)

            def norm2_stats(b):
                wait_apart(dve, x1_ready, b + 1)
                norm_stats(1, x1, norm2_chain)

            def norm2_apply(b, firsts):
                wait(dve, xn_transposed, firsts)
                norm_apply(1, b, x1, zn, norm2_chain, zn_ready)

            def mix(b):
                wait(dve, z_step_ready, b + 1)
                wait(dve, fr_projected, b)
                for out, c in ((z_k, 4), (z_r, 3)):
                    ins = nc.vector.scalar_tensor_tensor(
                        out=out[:, :], in0=z_step[:, :], scalar=col_sb[:, c:c + 1], in1=z_t[:, 0:LEN],
                        op0=ALU.mult, op1=ALU.add)
                ins.then_inc(z_mixed, 1)

            def gate_v(b):
                wait(dve, y_stored, 16 * b)
                wait(dve, gate_ready, b + 1)
                wait(dve, fv_projected, b + 1)
                nc.vector.scalar_tensor_tensor(
                    out=gated[:, :, :].rearrange("p a b -> p (a b)"),
                    in0=gate[:, :, :].rearrange("p a b -> p (a b)"), scalar=1.0, in1=ps_misc[:, :],
                    op0=ALU.add, op1=ALU.mult).then_inc(gated_ready, 1)

            def constant_rows():
                link(nc.vector.tensor_copy(cv[:, 0:1], rb_sb[:, 0:1]))
                link(nc.vector.tensor_copy(cv[:, 1:2], rb_sb[:, BUCKETS - 1:BUCKETS]))
                link(nc.vector.tensor_copy(cv[:, 2:3], rb_lim[:, 2:3]))
                for part in range(3):
                    link(nc.vector.tensor_copy(cv_parts[:, part, :], cv[:, :]))
                    if part < 2:
                        link(nc.vector.tensor_tensor(cv[:, :], cv[:, :], cv_parts[:, part, :], ALU.subtract))
                for part in range(3):
                    for kb in range(NB):
                        band_end = min(kb * P + BAND, LEN)
                        for kind, a, b in ((0, 0, kb * P), (2, kb * P, band_end), (1, band_end, LEN)):
                            if a < b:
                                ins = nc.vector.tensor_copy(
                                    const_rows[:, part, kb * LEN + a:kb * LEN + b],
                                    cv_parts[:, part, kind:kind + 1].to_broadcast([HEADS, b - a]))
                ins.then_inc(const_rows_ready, 1)

            def prologue():
                link(nc.vector.memset(q_stack[:, :, :].bitcast(F32), 0.0))
                nc.vector.memset(ones_row[:, :], 1.0).then_inc(bv_wide_ready, 1)
                norm1_stats(0)
                norm_moments(0, 0, norm1_chain)
                norm_rstd(0, 0, norm1_chain)
                norm1_apply(0)
                dve.wait_ge(rb_loaded, 16)
                link(nc.vector.tensor_reduce(rb_lim[:, 0:1], rb_sb[:, :], AX_X, ALU.max))
                link(nc.vector.tensor_reduce(rb_lim[:, 1:2], rb_sb[:, :], AX_X, ALU.min))
                link(nc.vector.tensor_tensor(rb_lim[:, 2:3], rb_lim[:, 0:1], rb_lim[:, 1:2], ALU.add))
                link(nc.vector.tensor_scalar(rb_lim[:, 2:3], rb_lim[:, 2:3], 0.5, None, ALU.mult))
                nc.vector.tensor_scalar(rb_c[:, :], rb_sb[:, :], rb_lim[:, 2:3], None,
                                        ALU.subtract).then_inc(centre_ready, 1)
                for k, near, far in bucket_ranges(1 - LEN, LEN):
                    a, b = near + LEN - 1, far + LEN
                    ins = nc.vector.tensor_copy(bias_line[:, a:b], rb_sb[:, k:k + 1].to_broadcast([HEADS, b - a]))
                ins.then_inc(lines_ready, 1)
                dve.wait_ge(weights_loaded, 48)
                nc.vector.tensor_copy(bv_wide[:, :], col_sb[:, 2:3].to_broadcast([P, P])).then_inc(bv_wide_ready, 1)
                nc.vector.tensor_scalar(qk_bias[:, 0:1], col_sb[:, 0:1], float(HD) ** -0.5, None, ALU.mult)
                nc.vector.tensor_copy(qk_bias[:, 1:2], col_sb[:, 1:2]).then_inc(qk_bias_ready, 1)
                nc.vector.tensor_scalar(w_sb[:, FV, :], w_sb[:, FV, :], 0.5, None, ALU.mult).then_inc(fv_halved, 1)
                constant_rows()
                dve.sem_inc(stacks_zeroed, 1)
                low_part(0, 0)
                low_part(0, 1)
                for u in range(2):
                    dve.wait_ge(bias_loaded[u], 16)
                    for n in range(4 * GH):
                        maximum(u, 4 * u + n // NB, n % NB, n)

            def iteration(i, first=False, last=False):
                for g in range(GROUPS):
                    w = 4 * i + g
                    if first and g < 2:
                        dve.wait_ge(bias_loaded[g + 2], 16)
                    for s in range(STEPS):
                        at = STEPS * g + s
                        if not last:
                            if at == DVE_AT["stats1"]:
                                norm1_stats(i + 1)
                            if at == DVE_AT["moments1"]:
                                norm_moments(0, i + 1, norm1_chain)
                            if at == DVE_AT["norm1"]:
                                norm1_apply(i + 1)
                            if at == DVE_AT["q_low"]:
                                low_part(i + 1, 0)
                            if at == DVE_AT["k_low"]:
                                low_part(i + 1, 1)
                        if at == DVE_AT["v"]:
                            if first:
                                dve.wait_ge(v_ones_ready, 1)
                            place_v(i)
                        if not first:
                            if at == DVE_AT["invert"]:
                                invert_sums(i - 1)
                            if at == DVE_AT["norm_o"]:
                                norm_o(i - 1)
                            if at == DVE_AT["residual"]:
                                add_residual(i - 1)
                                norm2_stats(i - 1)
                            if at == DVE_AT["moments2"]:
                                norm_moments(1, i - 1, norm2_chain)
                            if at == DVE_AT["norm2"]:
                                norm2_apply(i - 1, i + 1 if last else i + 2)
                            if at == DVE_AT["mix"]:
                                mix(i - 1)
                            if at == DVE_AT["gate"]:
                                gate_v(i - 1)
                        for n in (2 * s, 2 * s + 1):
                            if not last or g < 2:
                                maximum(w + 2, 4 * ((g + 2) % 4) + n // NB, n % NB, n)
                            if n == 2 * s:
                                if at == DVE_AT["rstd1"] and not last:
                                    norm_rstd(0, i + 1, norm1_chain)
                                if at == DVE_AT["rstd2"] and not first:
                                    norm_rstd(1, i - 1, norm2_chain)

            def epilogue():
                b = BATCH - 1
                invert_sums(b)
                norm_o(b)
                add_residual(b)
                norm2_stats(b)
                norm_moments(1, b, norm2_chain)
                norm_rstd(1, b, norm2_chain)
                norm2_apply(b, BATCH)
                mix(b)
                gate_v(b)

            run(dve, prologue, iteration, epilogue)

        @block.gpsimd
        def _(pool):
            chain = [0]

            def link(ins):
                chain[0] += 1
                ins.then_inc(setup_pool, 1)
                pool.wait_ge(setup_pool, chain[0])

            def weight_band(w, g, n, j):
                wait(pool, exped, STEPS * w + 2 * j + 2)
                period = LEN + P
                band = probs[n][:, j, 0:3 * period].rearrange("p (k q) -> p k q", q=period)[:, :, 0:BAND]
                nc.gpsimd.tensor_tensor(band, band, band_w[:, 4 * g + j, :].unsqueeze(1).broadcast_to([P, 3, BAND]),
                                        ALU.mult)
                corner = probs[n][:, j, 3 * period:NB * LEN]
                nc.gpsimd.tensor_tensor(corner, corner, band_w[:, 4 * g + j, 0:P], ALU.mult).then_inc(banded, 1)

            def split_shift(u, n):
                wait(pool, shift_copied, u + 1)
                nc.gpsimd.tensor_tensor(shift_parts[n][:, 1, :], shift_f[:, :], shift_parts[n][:, 0, :],
                                        ALU.subtract).then_inc(shift_split, 1)

            def less_high(b, t):
                wait(pool, qk_copied, 2 * b + t + 1)
                nc.gpsimd.tensor_tensor(qk_f[:, t, :], qk_f[:, t, :], parts[:, t, 0, :],
                                        ALU.subtract).then_inc(qk_less_high, 1)

            def bias_x_res(b):
                wait(pool, x_res_loaded, 16 * (b + 1))
                nc.gpsimd.tensor_tensor(x_res[:, :, :], x_res[:, :, :],
                                        proj_bias[:, :].unsqueeze(1).broadcast_to([P, NB, DIM]),
                                        ALU.add).then_inc(x_res_biased, 1)

            def step_z(b):
                wait(pool, z_mixed, b)
                wait(pool, z_t_ready, b + 1)
                nc.gpsimd.tensor_tensor(z_step[:, :], z_t[:, 1:LEN + 1], z_t[:, 0:LEN],
                                        ALU.subtract).then_inc(z_step_ready, 1)

            def square_k(b):
                wait(pool, fv_projected, b)
                wait(pool, k_relu_ready, b + 1)
                nc.gpsimd.tensor_tensor(k_act[:, :], k_relu[:, :], k_relu[:, :], ALU.mult).then_inc(k_act_ready, 1)

            def finish_y(b):
                wait(pool, gated_ready, b + 1)
                nc.gpsimd.tensor_tensor(y_sb[:, :, :], gated[:, :, :], x1[:, :, :], ALU.add).then_inc(y_ready, 1)

            def prologue():
                link(nc.gpsimd.memset(ident[:, :], 0.0))
                nc.gpsimd.affine_select(out=ident[:, :], in_=ident[:, :], compare_op=ALU.not_equal, fill=1.0,
                                        base=0, pattern=[[-1, P]], channel_multiplier=1).then_inc(ident_ready, 1)
                link(nc.gpsimd.memset(k_stack[:, :, :].bitcast(F32), 0.0))
                for r in range(3 * NB + 2):
                    a, b = (r % NB * P, (r % NB + 1) * P) if r < 3 * NB else (0, LEN)
                    rows = k_stack[CONST_ROW:P, 0, a:b]
                    link(nc.gpsimd.affine_select(out=rows, in_=rows, compare_op=ALU.not_equal, fill=1.0,
                                                 base=-r, pattern=[[0, b - a]], channel_multiplier=1))
                link(nc.gpsimd.tensor_copy(k_stack[CONST_ROW:P, 1:HEADS, :],
                                           k_stack[CONST_ROW:P, 0, :].unsqueeze(1).broadcast_to(
                                               [P - CONST_ROW, HEADS - 1, LEN])))
                pool.sem_inc(k_const_ready, 1)
                pool.sem_inc(stacks_zeroed, 1)
                pool.wait_ge(centre_ready, 1)
                for k, near, far in bucket_ranges(-P, BAND - 1):
                    a, b = BAND - 1 - far, BAND - near
                    ins = nc.gpsimd.tensor_copy(band_line[:, a:b], rb_c[:, k:k + 1].to_broadcast([HEADS, b - a]))
                ins.then_inc(lines_ready, 1)
                less_high(0, 0)
                less_high(0, 1)
                nc.gpsimd.memset(v_sb[:, :, :, :], 1.0).then_inc(v_ones_ready, 1)
                nc.gpsimd.memset(z_t[:, 0:1], 0.0).then_inc(z_zero_ready, 1)
                split_shift(0, 0)
                pool.wait_ge(z_zero_ready, 1)
                pool.wait_ge(band_ready, 1)
                pool.wait_ge(proj_bias_ready, 1)

            def iteration(i, first=False, last=False):
                for g in range(GROUPS):
                    w = 4 * i + g
                    for j in range(GH):
                        at = STEPS * g + 2 * j + 1
                        weight_band(w, g, g % 2, j)
                        if j == 0 and not (last and g == 3):
                            split_shift(w + 1, (g + 1) % 2)
                        if not last:
                            if at == POOL_AT["q_less"]:
                                less_high(i + 1, 0)
                            if at == POOL_AT["k_less"]:
                                less_high(i + 1, 1)
                        if not first:
                            if at == POOL_AT["x_res"]:
                                bias_x_res(i - 1)
                            if at == POOL_AT["z_step"]:
                                step_z(i - 1)
                            if at == POOL_AT["square"]:
                                square_k(i - 1)
                            if at == POOL_AT["y"]:
                                finish_y(i - 1)

            def epilogue():
                b = BATCH - 1
                bias_x_res(b)
                step_z(b)
                square_k(b)
                finish_y(b)

            run(pool, prologue, iteration, epilogue)


def kernel(**inputs):
    import numpy as np
    import concourse.bacc as bacc
    from concourse.bass_utils import run_bass_kernel_spmd

    attn = {n: np.asarray(inputs[f"L0_attn_{n}"]) for n in ("x", "wq", "bq", "wk", "bk", "wv", "bv", "wo", "bo", "rel_bias")}
    ffn = {n: np.asarray(inputs[f"L0_ffn_{n}"]) for n in ("W_r", "W_k", "W_v", "mu_r", "mu_k")}
    arrays = {
        "x": attn["x"].reshape(BATCH, NB, P, DIM).transpose(0, 2, 1, 3),
        "weights": np.stack([w.T for w in (attn["wq"], attn["wk"], attn["wv"], attn["wo"],
                                           ffn["W_r"], ffn["W_k"], ffn["W_v"])], axis=1),
        "columns": np.stack([attn["bq"], attn["bk"], attn["bv"], ffn["mu_r"], ffn["mu_k"]], axis=1),
        "bo_row": attn["bo"].reshape(1, DIM),
        "rel_bias_t": attn["rel_bias"].T,
    }
    arrays = {n: np.ascontiguousarray(a) for n, a in arrays.items()}
    nc = bacc.Bacc("TRN2", target_bir_lowering=False, num_devices=1)
    args = [nc.dram_tensor(n, a.shape, mybir.dt.from_np(a.dtype), kind="ExternalInput").ap() for n, a in arrays.items()]
    y = nc.dram_tensor("y", (BATCH, P, NB, DIM), F32, kind="ExternalOutput").ap()
    attention_ffn_program(nc, *args, y)
    got = run_bass_kernel_spmd(nc, [arrays], core_ids=[0])
    return got.results[0]["y"].transpose(0, 2, 1, 3).reshape(BATCH, LEN, DIM)
```

```python
import math
from contextlib import ExitStack

import concourse.bass as bass
from concourse import mybir

F32 = mybir.dt.float32
BF16 = mybir.dt.bfloat16
F16 = mybir.dt.float16
I32 = mybir.dt.int32
ALU = mybir.AluOpType
ACT = mybir.ActivationFunctionType
AX_X = mybir.AxisListType.X

P = 128
BATCH, LEN, DIM = 8, 512, 128
HEADS, HD = 16, 8
NB = LEN // P
GROUPS, GH = 4, 4
UNITS = BATCH * GROUPS
STEPS = 8
BUCKETS, MAX_DISTANCE = 32, 128
EPS = 1e-5
RSQRT_MAGIC = float(0x5F3759DF)
NEWTON_STEPS = 3
NORM_LINKS = 2 + 2 + 4 * NEWTON_STEPS

Q_PART = [0, 0, 0, 1, 1, 2]
K_PART = [1, 0, 2, 0, 1, 0]
SLOTS = len(Q_PART)
PARTS = 3
QK_ROWS = SLOTS * HD
MAX_PASS_ROWS = 96
CONST_ROW = 96
SHIFT_ROW = CONST_ROW + 3 * NB
EXP_PASS_ROWS = SHIFT_ROW + 2

LINE = 2 * LEN


def bucket_first(k):
    half = BUCKETS // 2
    if k < half:
        return k
    return math.ceil(half * (MAX_DISTANCE / half) ** ((k - half) / (BUCKETS - half)) - 1e-9)


def bucket_ranges(lowest, highest):
    firsts = [lowest] + [bucket_first(k) for k in range(1, BUCKETS)] + [highest + 1]
    for k in range(BUCKETS):
        a, b = max(firsts[k], lowest), min(firsts[k + 1] - 1, highest)
        if a <= b:
            yield k, a, b


BAND = P + bucket_first(BUCKETS - 1) - 1
BAND_LINE = BAND + P - 1
F16_MAX = 65504.0

P_V_STEPS = [1, 4, 5, 6]

PE_AT = dict(max0=0, norm1=2, q=3, k=6, max1=8, v=10, wo=15, max2=16, norm2=23, max3=25, fk=26, fr=27, fv=30)
ACT_AT = dict(max0=0, xn_t=1, q=3, k=6, q_mid=8, k_mid=8, max1=9, v=10, max2=16, z_t=23, max3=25, fk=26, fr=28)
DVE_AT = dict(stats1=23, moments1=26, v=8, invert=12, residual=16, moments2=18, mix=25, gate=31)
POOL_AT = dict(shift=2, q_less=5, k_less=6, q_low=7, k_low=8, x_res=9, norm_o=15, norm2=18, z_step=24, norm1=27,
               square=28, y=31)





def wait(eng, sem, value):
    if not isinstance(value, int) or value > 0:
        eng.wait_ge(sem, value)


def attention_ffn_program(nc, x, weights, columns, bo_row, rel_bias_t, y):
    ctx = ExitStack()
    with ctx:
        def sb(name, shape, dt=F32):
            return ctx.enter_context(nc.sbuf_tensor(name, shape, dt))

        def psum(name, shape):
            return ctx.enter_context(nc.psum_tensor(name, shape, F32))

        def sem(name):
            return ctx.enter_context(nc.semaphore(name))

        bias_line_dram = nc.dram_tensor("bias_line_dram", (HEADS, LINE), BF16, kind="Internal").ap()
        band_line_dram = nc.dram_tensor("band_line_dram", (2, HEADS, BAND_LINE), F16, kind="Internal").ap()
        image = [nc.dram_tensor(f"{n}_image", (HEADS, QK_ROWS, LEN), BF16, kind="Internal").ap() for n in "qk"]
        const_rows_dram = nc.dram_tensor("const_rows_dram", (HEADS, 3 * NB, LEN), BF16, kind="Internal").ap()
        sums_dram = nc.dram_tensor("sums_dram", (HEADS, LEN), F32, kind="Internal").ap()
        inverse_dram = nc.dram_tensor("inverse_dram", (HEADS, LEN), F32, kind="Internal").ap()

        w_sb = sb("w_sb", [P, 7, DIM])
        WQ, WK, WV, WO, FR, FK, FV = range(7)
        col_sb = sb("col_sb", [P, 5])
        bo_sb = sb("bo_sb", [1, DIM])
        ones_row = sb("ones_row", [1, P])
        ident = sb("ident", [P, P])
        bv_wide = sb("bv_wide", [P, P])
        qk_bias = sb("qk_bias", [P, 2])
        proj_bias = sb("proj_bias", [P, DIM])
        q_stack = sb("q_stack", [P, HEADS, LEN], BF16)
        k_stack = sb("k_stack", [P, HEADS, LEN], BF16)
        bias_tab = sb("bias_tab", [P, HEADS, 2 * LEN - P], BF16)
        band_tab = sb("band_tab", [P, 2, HEADS, BAND], F16)
        ident16 = sb("ident16", [P, P], F16)
        rb_parts = sb("rb_parts", [HEADS, 2, BUCKETS], F16)
        probs = [sb(f"probs{n}", [P, GH, NB * LEN]) for n in range(2)]
        v_sb = sb("v_sb", [P, NB, HEADS, 32])
        v_stage = sb("v_stage", [P, NB * DIM])
        maxes = [sb(f"maxes{n}", [P, GH * NB]) for n in range(2)]
        shift_f = sb("shift_f", [GH * NB, P])
        shift_parts = [sb(f"shift_parts{n}", [GH * NB, 2, P], BF16) for n in range(2)]
        x_in = sb("x_in", [P, NB, DIM])
        xn = sb("xn", [P, NB, DIM])
        xn_t = sb("xn_t", [P, LEN])
        qk_f = sb("qk_f", [P, 2, LEN])
        parts = sb("parts", [P, 2, 3, LEN], BF16)
        o_t = [sb(f"o_t{n}", [P, LEN]) for n in range(2)]
        numer = sb("numer", [P, LEN])
        inverse = sb("inverse", [P, LEN])
        sums = sb("sums", [P, HEADS * LEN // P])
        x_res = sb("x_res", [P, NB, DIM])
        x1 = sb("x1", [P, NB, DIM])
        zn = xn
        z_t = sb("z_t", [P, LEN + 1])
        z_step = sb("z_step", [P, LEN])
        z_k = sb("z_k", [P, LEN])
        z_r = sb("z_r", [P, LEN])
        k_relu = sb("k_relu", [P, LEN])
        k_act = sb("k_act", [P, LEN])
        gate = sb("gate", [P, NB, DIM])
        gated = sb("gated", [P, NB, DIM])
        y_sb = gated
        stats = [sb(f"stats{n}", [P, NB, 6]) for n in range(2)]
        moments = [sb(f"moments{n}", [P, NB, 2]) for n in range(2)]
        rstd = [sb(f"rstd{n}", [P, NB]) for n in range(2)]
        variance = [sb(f"variance{n}", [P, NB]) for n in range(2)]
        newton = [sb(f"newton{n}", [P, NB]) for n in range(2)]
        rb_sb = sb("rb_sb", [HEADS, BUCKETS])
        rb_c = sb("rb_c", [HEADS, BUCKETS])
        rb_lim = sb("rb_lim", [HEADS, 3])
        cv = sb("cv", [HEADS, 3])
        cv_parts = sb("cv_parts", [HEADS, 3, 3], BF16)
        bias_line = probs[0][0:HEADS, 0, 0:LINE // 2].bitcast(BF16)
        band_line = probs[0][0:HEADS, 1, 0:BAND_LINE].bitcast(F16).rearrange("h (c m) -> h c m", c=2)
        const_rows = probs[1][0:HEADS, 0:3, 0:NB * LEN // 2].bitcast(BF16)

        ps_max = [psum(f"ps_max{n}", [P, LEN]) for n in range(2)]
        ps_exp = [psum(f"ps_exp{n}", [P, 2, LEN]) for n in range(2)]
        ps_out = psum("ps_out", [P, LEN])
        ps_misc = psum("ps_misc", [P, LEN])

        weights_loaded, rb_loaded = sem("weights_loaded"), sem("rb_loaded")
        setup_dve, setup_pool = sem("setup_dve"), sem("setup_pool")
        bv_wide_ready = sem("bv_wide_ready")
        bias_line_ready, bias_line_stored = sem("bias_line_ready"), sem("bias_line_stored")
        band_line_ready, band_line_stored = sem("band_line_ready"), sem("band_line_stored")
        bias_loaded = [sem(f"bias_loaded{g}") for g in range(GROUPS)]
        band_loaded = sem("band_loaded")
        const_rows_ready, const_rows_stored, const_rows_loaded = (
            sem("const_rows_ready"), sem("const_rows_stored"), sem("const_rows_loaded"))
        k_const_built, k_const_loaded = sem("k_const_built"), sem("k_const_loaded")
        stacks_zeroed, ident_ready = sem("stacks_zeroed"), sem("ident_ready")
        v_ones_ready, z_zero_ready = sem("v_ones_ready"), sem("z_zero_ready")
        centre_ready = sem("centre_ready")
        proj_bias_done, proj_bias_ready = sem("proj_bias_done"), sem("proj_bias_ready")
        qk_bias_ready, fv_halved = sem("qk_bias_ready"), sem("fv_halved")
        x_loaded, norm1_chain, xn_ready = sem("x_loaded"), sem("norm1_chain"), sem("xn_ready")
        xn_transposed, xn_t_ready = sem("xn_transposed"), sem("xn_t_ready")
        qk_projected, qk_copied = sem("qk_projected"), sem("qk_copied")
        qk_less_high, qk_mid_ready, qk_split = sem("qk_less_high"), sem("qk_mid_ready"), sem("qk_split")
        image_written = [sem("q_image_written"), sem("k_image_written")]
        stacks_loaded = [sem(f"stacks_loaded{g}") for g in range(GROUPS)]
        v_projected, v_staged, v_ready = sem("v_projected"), sem("v_staged"), sem("v_ready")
        max_scored, maxed = sem("max_scored"), sem("maxed")
        max_transposed, shift_copied, shift_split = sem("max_transposed"), sem("shift_copied"), sem("shift_split")
        shift_loaded = [sem(f"shift_loaded{n}") for n in range(2)]
        exp_scored, exped = sem("exp_scored"), sem("exped")
        pv_done, o_copied = sem("pv_done"), sem("o_copied")
        o_moved = [sem(f"o_moved{n}") for n in range(2)]
        sums_stored = [sem(f"sums_stored{n}") for n in range(2)]
        sums_loaded, inverted, inverse_stored = sem("sums_loaded"), sem("inverted"), sem("inverse_stored")
        inverse_loaded, o_normed = sem("inverse_loaded"), sem("o_normed")
        x_res_loaded, x_res_biased, attn_projected, x1_ready = (
            sem("x_res_loaded"), sem("x_res_biased"), sem("attn_projected"), sem("x1_ready"))
        norm2_chain, zn_ready, zn_transposed, z_t_ready = (
            sem("norm2_chain"), sem("zn_ready"), sem("zn_transposed"), sem("z_t_ready"))
        z_step_ready, z_mixed = sem("z_step_ready"), sem("z_mixed")
        fk_projected, k_relu_ready, k_act_ready = sem("fk_projected"), sem("k_relu_ready"), sem("k_act_ready")
        fr_projected, gate_ready, fv_projected, gated_ready = (
            sem("fr_projected"), sem("gate_ready"), sem("fv_projected"), sem("gated_ready"))
        y_ready, y_stored = sem("y_ready"), sem("y_stored")

        waits_apart = sem("waits_apart")

        def wait_apart(eng, sem_, value):
            if isinstance(value, int):
                wait(eng, sem_, value)
            else:
                eng.wait_ge(sem_, value)
                eng.sem_inc(waits_apart, 1)

        def turn(b, g):
            return 2 * b + g // 2

        block = ctx.enter_context(nc.Block())

        def run(eng, prologue, iteration, epilogue, alike=BATCH - 4):
            prologue()
            iteration(0, first=True)
            iteration(1)
            with eng.Fori(2, 2 + alike) as i:
                iteration(i)
            for i in range(2 + alike, BATCH):
                iteration(i, last=i == BATCH - 1)
            epilogue()

        def has_norm1(i):
            return not isinstance(i, int) or i + 2 < BATCH

        def norm_rstd(eng, ops, k, b, done):
            var, r, t = variance[k], rstd[k], newton[k]
            steps = [lambda: ops.tensor_scalar(var[:, :], moments[k][:, :, 1], EPS, None, ALU.add),
                     lambda: ops.tensor_scalar(r[:, :].bitcast(I32), var[:, :].bitcast(I32), -0.5,
                                                     RSQRT_MAGIC, ALU.mult, ALU.add)]
            steps += NEWTON_STEPS * [
                lambda: ops.tensor_tensor(t[:, :], r[:, :], r[:, :], ALU.mult),
                lambda: ops.tensor_tensor(t[:, :], t[:, :], var[:, :], ALU.mult),
                lambda: ops.tensor_scalar(t[:, :], t[:, :], -0.5, 1.5, ALU.mult, ALU.add),
                lambda: ops.tensor_tensor(r[:, :], r[:, :], t[:, :], ALU.mult)]
            for n, step in enumerate(steps):
                wait_apart(eng, done, NORM_LINKS * b + 2 + n)
                step().then_inc(done, 1)

        def norm_apply(eng, ops, k, b, tile, out, done, ready):
            wait_apart(eng, done, NORM_LINKS * (b + 1))
            for blk in range(NB):
                ins = ops.tensor_scalar(out[:, blk, :], tile[:, blk, :], moments[k][:, blk, 0:1],
                                              rstd[k][:, blk:blk + 1], ALU.subtract, ALU.mult)
            ins.then_inc(ready, 1)

        def norm1(eng, ops, b):
            norm_rstd(eng, ops, 0, b, norm1_chain)
            wait_apart(eng, zn_transposed, b - 2)
            wait_apart(eng, xn_transposed, b)
            norm_apply(eng, ops, 0, b, x_in, xn, norm1_chain, xn_ready)

        def norm2(eng, ops, b, firsts):
            norm_rstd(eng, ops, 1, b, norm2_chain)
            wait_apart(eng, xn_transposed, firsts)
            norm_apply(eng, ops, 1, b, x1, zn, norm2_chain, zn_ready)

        def norm_o(eng, ops, b):
            for n in range(2):
                wait(eng, o_moved[n], 128 * (b + 1))
            wait(eng, inverse_loaded, 16 * (b + 1))
            ops.tensor_tensor(numer[:, :], numer[:, :], inverse[:, :], ALU.mult).then_inc(o_normed, 1)

        def bias_x_res(eng, ops, b):
            wait(eng, x_res_loaded, 16 * (b + 1))
            ops.tensor_tensor(x_res[:, :, :], x_res[:, :, :],
                                    proj_bias[:, :].unsqueeze(1).broadcast_to([P, NB, DIM]),
                                    ALU.add).then_inc(x_res_biased, 1)

        def step_z(eng, ops, b):
            wait(eng, z_mixed, b)
            wait(eng, z_t_ready, b + 1)
            ops.tensor_tensor(z_step[:, :], z_t[:, 1:LEN + 1], z_t[:, 0:LEN],
                                    ALU.subtract).then_inc(z_step_ready, 1)

        def square_k(eng, ops, b):
            wait(eng, fv_projected, b)
            wait(eng, k_relu_ready, b + 1)
            ops.tensor_tensor(k_act[:, :], k_relu[:, :], k_relu[:, :], ALU.mult).then_inc(k_act_ready, 1)

        def finish_y(eng, ops, b):
            wait(eng, gated_ready, b + 1)
            ops.tensor_tensor(y_sb[:, :, :], gated[:, :, :], x1[:, :, :], ALU.add).then_inc(y_ready, 1)


        @block.sync
        def _(sp):
            def load_x(b):
                wait_apart(sp, xn_ready, b)
                sp.dma_start(x_in[:, :, :], x[b]).then_inc(x_loaded, 16)

            def load_bias_tab(g):
                sp.dma_start(bias_tab[:, 4 * g:4 * g + 4, :], bass.AP(bias_line_dram.tensor, 4 * g * LINE, [
                    [1, P], [LINE, GH], [1, 2 * LEN - P]])).then_inc(bias_loaded[g], 16)

            def load_band_tab(part):
                sp.dma_start(band_tab[:, part, :, :], bass.AP(
                    band_line_dram.tensor, part * HEADS * BAND_LINE, [
                        [1, P], [BAND_LINE, HEADS], [1, BAND]])).then_inc(band_loaded, 16)

            def write_image(b, t):
                wait_apart(sp, qk_split, 2 * b + t + 1)
                for g in range(GROUPS):
                    wait_apart(sp, stacks_loaded[g], 32 * b)
                for part in range(PARTS):
                    slots = [s for s in range(SLOTS) if (Q_PART, K_PART)[t][s] == part]
                    apart = slots[1] - slots[0] if len(slots) > 1 else 1
                    rows = image[t].rearrange("h (d s) t -> (h d) s t", s=SLOTS)[:, slots[0]:slots[-1] + 1:apart, :]
                    sp.dma_start(rows, parts[:, t, part, :].unsqueeze(1).broadcast_to([P, len(slots), LEN])
                                 ).then_inc(image_written[t], 16)

            def load_stacks(b, g):
                u = 4 * b + g
                wait_apart(sp, image_written[0], 16 * PARTS * (b + 1))
                wait_apart(sp, image_written[1], 16 * PARTS * (b + 1))
                wait_apart(sp, exp_scored, STEPS * (u - GROUPS + 1))
                for stack, im in ((q_stack, image[0]), (k_stack, image[1])):
                    sp.dma_start(stack[0:QK_ROWS, 4 * g:4 * g + 4, :],
                                 im[4 * g:4 * g + 4].rearrange("h r t -> r h t")).then_inc(stacks_loaded[g], 16)

            def load_shift(b, g):
                wait_apart(sp, shift_split, 4 * b + g + 1)
                for part in range(2):
                    sp.dma_start(q_stack[SHIFT_ROW + part:SHIFT_ROW + part + 1, 4 * g:4 * g + 4, :],
                                 shift_parts[g % 2][:, part, :]).then_inc(shift_loaded[g % 2], 16)

            def move_o(b, g):
                u = 4 * b + g
                wait_apart(sp, o_copied, u + 1)
                if g == 0:
                    wait_apart(sp, attn_projected, b)
                    wait_apart(sp, sums_loaded, 16 * b)
                sp.dma_start(sums_dram[4 * g:4 * g + 4, :],
                             o_t[g % 2][HD:P:32, :]).then_inc(sums_stored[g % 2], 16)
                for j in range(GH):
                    sp.dma_start(numer[32 * g + 8 * j:32 * g + 8 * j + 8, :],
                                 o_t[g % 2][32 * j:32 * j + HD, :]).then_inc(o_moved[g % 2], 16)

            def load_sums(b):
                for n in range(2):
                    wait_apart(sp, sums_stored[n], 32 * (b + 1))
                wait_apart(sp, inverse_stored, 16 * b)
                sp.dma_start(sums[:, :], sums_dram.rearrange("h (r c) -> (h r) c", c=HEADS * LEN // P)
                             ).then_inc(sums_loaded, 16)

            def store_inverse(b):
                wait_apart(sp, inverted, b + 1)
                wait_apart(sp, inverse_loaded, 16 * b)
                sp.dma_start(inverse_dram.rearrange("h (r c) -> (h r) c", c=HEADS * LEN // P),
                             sums[:, :]).then_inc(inverse_stored, 16)

            def load_inverse(b):
                wait_apart(sp, inverse_stored, 16 * (b + 1))
                wait_apart(sp, o_normed, b)
                sp.dma_start(inverse[:, :], bass.AP(inverse_dram.tensor, 0, [[LEN, HEADS], [0, HD], [1, LEN]])
                             ).then_inc(inverse_loaded, 16)

            def load_x_res(b):
                wait_apart(sp, x1_ready, b)
                sp.dma_start(x_res[:, :, :], x[b]).then_inc(x_res_loaded, 16)

            def store_y(b):
                wait_apart(sp, y_ready, b + 1)
                sp.dma_start(y[b], y_sb[:, :, :]).then_inc(y_stored, 16)

            def prologue():
                load_x(0)
                sp.dma_start(rb_sb[:, :], rel_bias_t).then_inc(rb_loaded, 16)
                sp.dma_start(w_sb[:, :, :], weights).then_inc(weights_loaded, 16)
                sp.dma_start(col_sb[:, :], columns).then_inc(weights_loaded, 16)
                sp.dma_start(bo_sb[:, :], bo_row).then_inc(weights_loaded, 16)
                sp.wait_ge(bias_line_ready, 1)
                sp.dma_start(bias_line_dram, bias_line).then_inc(bias_line_stored, 16)
                sp.wait_ge(bias_line_stored, 16)
                load_bias_tab(0)
                load_x(1)
                sp.wait_ge(const_rows_ready, 1)
                sp.dma_start(const_rows_dram.rearrange("h (p k) t -> h p (k t)", p=3), const_rows
                             ).then_inc(const_rows_stored, 16)
                sp.wait_ge(band_line_ready, 1)
                sp.dma_start(band_line_dram.rearrange("c h m -> h c m"), band_line).then_inc(band_line_stored, 16)
                sp.wait_ge(band_line_stored, 16)
                load_band_tab(0)
                write_image(0, 0)
                write_image(0, 1)
                sp.wait_ge(stacks_zeroed, 2)
                load_stacks(0, 0)
                load_stacks(0, 1)
                load_bias_tab(1)
                load_band_tab(1)
                sp.wait_ge(const_rows_stored, 16)
                sp.dma_start(q_stack[CONST_ROW:CONST_ROW + 3 * NB, :, :],
                             const_rows_dram.rearrange("h r t -> r h t")).then_inc(const_rows_loaded, 16)
                sp.wait_ge(k_const_built, 1)
                sp.dma_start(k_stack[CONST_ROW:EXP_PASS_ROWS, 1:HEADS, :],
                             k_stack[CONST_ROW:EXP_PASS_ROWS, 0, :].unsqueeze(1).broadcast_to(
                                 [EXP_PASS_ROWS - CONST_ROW, HEADS - 1, LEN])).then_inc(k_const_loaded, 16)
                load_stacks(0, 2)
                load_bias_tab(2)
                load_stacks(0, 3)
                load_bias_tab(3)
                load_shift(0, 0)

            def iteration(i, first=False, last=False):
                if not first:
                    move_o(i - 1, 2)
                    load_stacks(i, 3)
                load_shift(i, 1)
                if has_norm1(i):
                    load_x(i + 2)
                if not first:
                    load_x_res(i - 1)
                if not first:
                    move_o(i - 1, 3)
                    load_sums(i - 1)
                if not last:
                    write_image(i + 1, 0)
                load_shift(i, 2)
                if not first:
                    store_inverse(i - 1)
                if not last:
                    write_image(i + 1, 1)
                if not first:
                    load_inverse(i - 1)
                if not last:
                    load_stacks(i + 1, 0)
                move_o(i, 0)
                if not last:
                    load_stacks(i + 1, 1)
                load_shift(i, 3)
                move_o(i, 1)
                if not last:
                    load_stacks(i + 1, 2)
                    load_shift(i + 1, 0)
                if not first and not last:
                    store_y(i - 1)

            def epilogue():
                move_o(BATCH - 1, 2)
                store_y(BATCH - 2)
                load_x_res(BATCH - 1)
                move_o(BATCH - 1, 3)
                load_sums(BATCH - 1)
                store_inverse(BATCH - 1)
                load_inverse(BATCH - 1)
                store_y(BATCH - 1)
                sp.wait_ge(y_stored, 16 * BATCH)

            run(sp, prologue, iteration, epilogue)

        @block.tensor
        def _(pe):
            def max_scores(u, h, qb, n):
                number = 16 * u + n
                wait(pe, maxed, number - 1)
                pe.matmul(ps_max[n % 2][:, :], q_stack[0:MAX_PASS_ROWS, h, qb * P:(qb + 1) * P],
                          k_stack[0:MAX_PASS_ROWS, h, :], start=True, stop=True).then_inc(max_scored, 1)

            def exp_scores(w, h, s):
                wait(pe, exped, STEPS * w + s - 1)
                for n in range(2):
                    kb = 2 * (s % 2) + n
                    band = min(BAND, LEN - kb * P)
                    pe.matmul(ps_exp[s % 2][:, n, :], k_stack[0:EXP_PASS_ROWS, h, kb * P:(kb + 1) * P],
                              q_stack[0:EXP_PASS_ROWS, h, :], start=True, stop=False)
                    for part in range(2):
                        bias = bass.AP(band_tab, (part * HEADS + h) * BAND + BAND - 1,
                                       [[2 * HEADS * BAND, P], [-1, band]])
                        mm = pe.matmul(ps_exp[s % 2][:, n, kb * P:kb * P + band], ident16[:, :], bias,
                                       start=False, stop=part == 1)
                mm.then_inc(exp_scored, 1)

            def p_v(w, g, n, kb):
                if kb == 0:
                    wait(pe, exped, STEPS * (w + 1))
                    wait(pe, o_copied, w)
                for j in range(GH):
                    mm = pe.matmul(ps_out[32 * j:32 * j + 32, :], v_sb[:, kb, 4 * g + j, :],
                                   probs[n][:, j, kb * LEN:(kb + 1) * LEN], start=kb == 0, stop=kb == NB - 1)
                if kb == NB - 1:
                    mm.then_inc(pv_done, 1)

            def transpose_maxima(u, n):
                wait(pe, maxed, 16 * (u + 1))
                pe.matmul(ps_misc[0:GH * NB, 0:P], maxes[n][:, :], ident[:, :],
                          start=True, stop=True).then_inc(max_transposed, 1)

            def transposes(tile, ready, count, done):
                wait(pe, ready, count)
                for blk in range(NB):
                    mm = pe.transpose(ps_misc[:, blk * P:(blk + 1) * P], tile[:, blk, :], ident[:, :])
                mm.then_inc(done, 1)

            def channels_out(w, moving, done):
                pe.matmul(ps_misc[:, :], w_sb[:, w, :], moving, start=True, stop=True).then_inc(done, 1)

            def tokens_out(w, stationary, done):
                for blk in range(NB):
                    mm = pe.matmul(ps_misc[:, blk * DIM:(blk + 1) * DIM], stationary[:, blk * P:(blk + 1) * P],
                                   w_sb[:, w, :], start=True, stop=True)
                mm.then_inc(done, 1)

            def norm1_transposes(b):
                transposes(xn, xn_ready, b + 1, xn_transposed)

            def project_qk(b, t):
                if t == 0:
                    wait(pe, xn_t_ready, b + 1)
                else:
                    wait(pe, qk_copied, 2 * b + 1)
                channels_out((WQ, WK)[t], xn_t[:, :], qk_projected)

            def project_v(b):
                tokens_out(WV, xn_t, v_projected)

            def project_o(b):
                wait(pe, o_normed, b + 1)
                tokens_out(WO, numer, attn_projected)

            def norm2_transposes(b):
                transposes(zn, zn_ready, b + 1, zn_transposed)

            def ffn_k(b):
                wait(pe, z_mixed, b + 1)
                channels_out(FK, z_k[:, :], fk_projected)

            def ffn_r(b):
                wait(pe, k_relu_ready, b + 1)
                tokens_out(FR, z_r, fr_projected)

            def ffn_v(b):
                wait(pe, gate_ready, b + 1)
                wait(pe, k_act_ready, b + 1)
                tokens_out(FV, k_act, fv_projected)

            def prologue():
                pe.wait_ge(ident_ready, 2)
                norm1_transposes(0)
                pe.wait_ge(weights_loaded, 48)
                project_qk(0, 0)
                project_qk(0, 1)
                pe.wait_ge(qk_copied, 2)
                project_v(0)
                pe.wait_ge(bv_wide_ready, 2)
                pe.wait_ge(fv_halved, 1)
                pe.wait_ge(v_staged, 1)
                pe.matmul(ps_misc[:, 0:DIM], bv_wide[:, :], w_sb[:, WO, :], start=True, stop=False)
                pe.matmul(ps_misc[:, 0:DIM], ones_row[:, :], bo_sb[:, :],
                          start=False, stop=True).then_inc(proj_bias_done, 1)
                for u in range(2):
                    pe.wait_ge(stacks_loaded[u], 32)
                    for n in range(4 * GH):
                        max_scores(u, 4 * u + n // NB, n % NB, n)
                    if u == 0:
                        pe.wait_ge(proj_bias_ready, 1)
                        transpose_maxima(0, 0)

            def iteration(i, first=False, last=False):
                for g in range(GROUPS):
                    w = 4 * i + g
                    wait(pe, shift_loaded[g % 2], 32 * (turn(i, g) + 1))
                    maxima = not last or g < 2
                    if maxima:
                        wait(pe, stacks_loaded[(g + 2) % 4], 32 * (i + 1 + g // 2))
                    if first and g == 0:
                        pe.wait_ge(const_rows_loaded, 16)
                        pe.wait_ge(k_const_built, 1)
                        pe.wait_ge(k_const_loaded, 16)
                        pe.wait_ge(band_loaded, 32)
                    for s in range(STEPS):
                        at = STEPS * g + s
                        exp_scores(w, 4 * g + s // 2, s)
                        if maxima:
                            for n in (2 * s, 2 * s + 1):
                                max_scores(w + 2, 4 * ((g + 2) % 4) + n // NB, n % NB, n)
                        if s in P_V_STEPS and not (first and g == 0):
                            if g == 1 and s == P_V_STEPS[0]:
                                wait(pe, v_ready, i + 1)
                            p_v(w - 1, (g - 1) % 4, (g - 1) % 2, P_V_STEPS.index(s))
                        if at == PE_AT[f"max{g}"] and not (last and g == 3):
                            if g == 0 and not first:
                                wait(pe, gated_ready, i - 1)
                            elif g == 1 and not last:
                                wait(pe, qk_copied, 2 * i + 4)
                            elif g == 3 and not first:
                                wait(pe, z_t_ready, i)
                            elif g == 2 and first:
                                wait(pe, v_staged, i + 2)
                            elif g == 2:
                                wait(pe, x1_ready, i)
                            wait(pe, shift_copied, w + 1)
                            transpose_maxima(w + 1, (g + 1) % 2)
                        if not last:
                            if at == PE_AT["norm1"]:
                                wait(pe, shift_copied, w + 2)
                                norm1_transposes(i + 1)
                            if at == PE_AT["q"]:
                                project_qk(i + 1, 0)
                            if at == PE_AT["k"]:
                                project_qk(i + 1, 1)
                            if at == PE_AT["v"]:
                                wait(pe, shift_copied, w + 2)
                                project_v(i + 1)
                        if not first:
                            if at == PE_AT["wo"]:
                                if last:
                                    wait(pe, shift_copied, 4 * i + 3)
                                else:
                                    wait(pe, v_staged, i + 2)
                                project_o(i - 1)
                            if at == PE_AT["norm2"]:
                                wait(pe, shift_copied, w + 2)
                                norm2_transposes(i - 1)
                            if at == PE_AT["fk"]:
                                if last:
                                    wait(pe, z_t_ready, i)
                                else:
                                    wait(pe, shift_copied, w + 2)
                                ffn_k(i - 1)
                            if at == PE_AT["fr"]:
                                ffn_r(i - 1)
                            if at == PE_AT["fv"]:
                                ffn_v(i - 1)

            def epilogue():
                for kb in range(NB):
                    p_v(UNITS - 1, GROUPS - 1, 1, kb)
                b = BATCH - 1
                pe.wait_ge(gated_ready, b)
                project_o(b)
                norm2_transposes(b)
                pe.wait_ge(z_t_ready, b + 1)
                ffn_k(b)
                ffn_r(b)
                ffn_v(b)

            run(pe, prologue, iteration, epilogue)

        @block.scalar
        def _(act):
            def exponentials(w, n, s):
                if s == 0:
                    wait(act, pv_done, w - 1)
                wait(act, exp_scored, STEPS * w + s + 1)
                nc.scalar.activation(
                    probs[n][:, s // 2, (s % 2) * 2 * LEN:(s % 2 + 1) * 2 * LEN],
                    ps_exp[s % 2][:, :, :].rearrange("p a b -> p (a b)"), ACT.Exp).then_inc(exped, 1)

            def copy_o(b, g):
                n = g % 2
                wait(act, o_moved[n], 64 * turn(b, g))
                wait(act, sums_stored[n], 16 * turn(b, g))
                wait(act, pv_done, 4 * b + g + 1)
                nc.scalar.activation(o_t[n][:, :], ps_out[:, :], ACT.Copy).then_inc(o_copied, 1)

            def copy_shift(b, g):
                u, n = 4 * b + g, g % 2
                wait(act, shift_loaded[n], 32 * turn(b, g))
                wait(act, max_transposed, u + 1)
                nc.scalar.activation(shift_parts[n][:, 0, :], ps_misc[0:GH * NB, 0:P], ACT.Copy, scale=-1.0)
                wait(act, shift_split, u)
                nc.scalar.activation(shift_f[:, :], ps_misc[0:GH * NB, 0:P], ACT.Copy,
                                     scale=-1.0).then_inc(shift_copied, 1)

            def copy_xn_t(b):
                wait(act, xn_transposed, b + 1)
                nc.scalar.activation(xn_t[:, :], ps_misc[:, :], ACT.Copy).then_inc(xn_t_ready, 1)

            def copy_qk(b, t):
                wait(act, image_written[t], 16 * PARTS * b)
                wait(act, qk_split, 2 * b + t - 1)
                wait(act, qk_projected, 2 * b + t + 1)
                scale = (float(HD) ** -0.5, 1.0)[t]
                nc.scalar.activation(qk_f[:, t, :], ps_misc[:, :], ACT.Identity,
                                     bias=qk_bias[:, t:t + 1], scale=scale)
                nc.scalar.activation(parts[:, t, 0, :], ps_misc[:, :], ACT.Identity,
                                     bias=qk_bias[:, t:t + 1], scale=scale).then_inc(qk_copied, 1)

            def mid_part(b, t):
                wait(act, qk_less_high, 2 * b + t + 1)
                nc.scalar.activation(parts[:, t, 1, :], qk_f[:, t, :], ACT.Copy).then_inc(qk_mid_ready, 1)

            def stage_v(b):
                wait(act, v_ready, b)
                wait(act, v_projected, b + 1)
                nc.scalar.activation(v_stage[:, :], ps_misc[:, :], ACT.Copy).then_inc(v_staged, 1)

            def copy_z_t(b):
                wait(act, z_mixed, b)
                wait(act, zn_transposed, b + 1)
                nc.scalar.activation(z_t[:, 1:LEN + 1], ps_misc[:, :], ACT.Copy).then_inc(z_t_ready, 1)

            def relu_k(b):
                wait(act, k_act_ready, b)
                wait(act, fk_projected, b + 1)
                nc.scalar.activation(k_relu[:, :], ps_misc[:, :], ACT.Relu).then_inc(k_relu_ready, 1)

            def gate_tanh(b):
                wait(act, gated_ready, b)
                wait(act, fr_projected, b + 1)
                nc.scalar.activation(gate[:, :, :].rearrange("p a b -> p (a b)"), ps_misc[:, :], ACT.Tanh,
                                     scale=0.5).then_inc(gate_ready, 1)

            def prologue():
                copy_xn_t(0)
                act.wait_ge(qk_bias_ready, 1)
                for t in range(2):
                    copy_qk(0, t)
                stage_v(0)
                act.wait_ge(proj_bias_done, 1)
                nc.scalar.activation(proj_bias[:, :], ps_misc[:, 0:DIM], ACT.Copy).then_inc(proj_bias_ready, 1)
                for t in range(2):
                    mid_part(0, t)
                copy_shift(0, 0)
                act.wait_ge(const_rows_loaded, 16)

            def iteration(i, first=False, last=False):
                for g in range(GROUPS):
                    w = 4 * i + g
                    for s in range(STEPS):
                        at = STEPS * g + s
                        exponentials(w, g % 2, s)
                        if s == 0 and not (first and g < 2):
                            copy_o(i - 1 if g < 2 else i, (g + 2) % 4)
                        if last and at == 4 * STEPS - 2:
                            copy_o(i, 2)
                        if at == ACT_AT[f"max{g}"] and not (last and g == 3):
                            copy_shift(i + (g + 1) // 4, (g + 1) % 4)
                        if not last:
                            if at == ACT_AT["xn_t"]:
                                copy_xn_t(i + 1)
                            if at == ACT_AT["q"]:
                                copy_qk(i + 1, 0)
                            if at == ACT_AT["k"]:
                                copy_qk(i + 1, 1)
                            if at == ACT_AT["q_mid"]:
                                mid_part(i + 1, 0)
                            if at == ACT_AT["k_mid"]:
                                mid_part(i + 1, 1)
                            if at == ACT_AT["v"]:
                                stage_v(i + 1)
                        if not first:
                            if at == ACT_AT["z_t"]:
                                copy_z_t(i - 1)
                            if at == ACT_AT["fk"]:
                                relu_k(i - 1)
                            if at == ACT_AT["fr"]:
                                gate_tanh(i - 1)

            def epilogue():
                copy_o(BATCH - 1, 3)
                b = BATCH - 1
                copy_z_t(b)
                relu_k(b)
                gate_tanh(b)

            run(act, prologue, iteration, epilogue)

        @block.vector
        def _(dve):
            chain = [0]

            def link(ins):
                chain[0] += 1
                ins.then_inc(setup_dve, 1)
                dve.wait_ge(setup_dve, chain[0])

            def maximum(u, h, qb, n):
                if n == 0:
                    wait(dve, max_transposed, u - 1)
                wait_apart(dve, max_scored, 16 * u + n + 1)
                window = bass.AP(bias_tab, h * (2 * LEN - P) + LEN - 1 + qb * P,
                                 [[HEADS * (2 * LEN - P), P], [-1, LEN]])
                nc.vector.tensor_tensor_reduce(
                    ps_max[n % 2][:, :], ps_max[n % 2][:, :], window, 1.0, -3.0e38,
                    ALU.add, ALU.max, maxes[(h // GH) % 2][:, n:n + 1]).then_inc(maxed, 1)

            def norm_stats(k, tile, done):
                for blk in range(NB):
                    ins = nc.vector.bn_stats(stats[k][:, blk, :], tile[:, blk, :])
                ins.then_inc(done, 1)

            def norm_moments(k, b, done):
                wait_apart(dve, done, NORM_LINKS * b + 1)
                for blk in range(NB):
                    ins = nc.vector.bn_aggr(moments[k][:, blk, :], stats[k][:, blk, :])
                ins.then_inc(done, 1)

            def norm1_stats(b):
                wait_apart(dve, x_loaded, 16 * (b + 1))
                wait_apart(dve, xn_ready, b)
                norm_stats(0, x_in, norm1_chain)

            def place_v(b):
                wait(dve, v_staged, b + 1)
                wait(dve, pv_done, 4 * b)
                nc.vector.tensor_copy(v_sb[:, :, :, 0:HD], v_stage[:, :].rearrange(
                    "p (n h d) -> p n h d", n=NB, h=HEADS)).then_inc(v_ready, 1)

            def invert_sums(b):
                wait(dve, sums_loaded, 16 * (b + 1))
                nc.vector.reciprocal(sums[:, :], sums[:, :]).then_inc(inverted, 1)

            def add_residual(b):
                wait(dve, y_ready, b)
                wait(dve, x_res_biased, b + 1)
                wait(dve, attn_projected, b + 1)
                nc.vector.tensor_tensor(x1[:, :, :], ps_misc[:, :].rearrange("p (a b) -> p a b", a=NB),
                                        x_res[:, :, :], ALU.add).then_inc(x1_ready, 1)

            def norm2_stats(b):
                wait_apart(dve, x1_ready, b + 1)
                wait_apart(dve, zn_ready, b)
                norm_stats(1, x1, norm2_chain)

            def mix(b):
                wait(dve, z_step_ready, b + 1)
                wait(dve, fr_projected, b)
                for out, c in ((z_k, 4), (z_r, 3)):
                    ins = nc.vector.scalar_tensor_tensor(
                        out=out[:, :], in0=z_step[:, :], scalar=col_sb[:, c:c + 1], in1=z_t[:, 0:LEN],
                        op0=ALU.mult, op1=ALU.add)
                ins.then_inc(z_mixed, 1)

            def gate_v(b):
                wait(dve, y_stored, 16 * b)
                wait(dve, gate_ready, b + 1)
                wait(dve, fv_projected, b + 1)
                nc.vector.scalar_tensor_tensor(
                    out=gated[:, :, :].rearrange("p a b -> p (a b)"),
                    in0=gate[:, :, :].rearrange("p a b -> p (a b)"), scalar=1.0, in1=ps_misc[:, :],
                    op0=ALU.add, op1=ALU.mult).then_inc(gated_ready, 1)

            def constant_rows():
                link(nc.vector.tensor_copy(cv[:, 0:1], rb_sb[:, 0:1]))
                link(nc.vector.tensor_copy(cv[:, 1:2], rb_sb[:, BUCKETS - 1:BUCKETS]))
                link(nc.vector.tensor_copy(cv[:, 2:3], rb_lim[:, 2:3]))
                for part in range(3):
                    link(nc.vector.tensor_copy(cv_parts[:, part, :], cv[:, :]))
                    if part < 2:
                        link(nc.vector.tensor_tensor(cv[:, :], cv[:, :], cv_parts[:, part, :], ALU.subtract))
                for part in range(3):
                    for kb in range(NB):
                        band_end = min(kb * P + BAND, LEN)
                        for kind, a, b in ((0, 0, kb * P), (2, kb * P, band_end), (1, band_end, LEN)):
                            if a < b:
                                ins = nc.vector.tensor_copy(
                                    const_rows[:, part, kb * LEN + a:kb * LEN + b],
                                    cv_parts[:, part, kind:kind + 1].to_broadcast([HEADS, b - a]))
                ins.then_inc(const_rows_ready, 1)

            def prologue():
                link(nc.vector.memset(q_stack[:, :, :].bitcast(F32), 0.0))
                dve.sem_inc(stacks_zeroed, 1)
                nc.vector.memset(ones_row[:, :], 1.0).then_inc(bv_wide_ready, 1)
                norm1_stats(0)
                norm_moments(0, 0, norm1_chain)
                norm1(dve, nc.vector, 0)
                dve.wait_ge(rb_loaded, 16)
                link(nc.vector.tensor_reduce(rb_lim[:, 0:1], rb_sb[:, :], AX_X, ALU.max))
                link(nc.vector.tensor_reduce(rb_lim[:, 1:2], rb_sb[:, :], AX_X, ALU.min))
                link(nc.vector.tensor_tensor(rb_lim[:, 2:3], rb_lim[:, 0:1], rb_lim[:, 1:2], ALU.add))
                link(nc.vector.tensor_scalar(rb_lim[:, 2:3], rb_lim[:, 2:3], 0.5, None, ALU.mult))
                link(nc.vector.tensor_scalar(rb_c[:, :], rb_sb[:, :], rb_lim[:, 2:3], None, ALU.subtract))
                link(nc.vector.tensor_scalar(rb_c[:, :], rb_c[:, :], F16_MAX, -F16_MAX, ALU.min, ALU.max))
                link(nc.vector.tensor_copy(rb_parts[:, 0, :], rb_c[:, :]))
                nc.vector.tensor_tensor(rb_parts[:, 1, :], rb_c[:, :], rb_parts[:, 0, :],
                                        ALU.subtract).then_inc(centre_ready, 1)
                for k, near, far in bucket_ranges(1 - LEN, LEN):
                    a, b = near + LEN - 1, far + LEN
                    ins = nc.vector.tensor_copy(bias_line[:, a:b], rb_sb[:, k:k + 1].to_broadcast([HEADS, b - a]))
                ins.then_inc(bias_line_ready, 1)
                dve.wait_ge(weights_loaded, 48)
                nc.vector.tensor_copy(bv_wide[:, :], col_sb[:, 2:3].to_broadcast([P, P])).then_inc(bv_wide_ready, 1)
                nc.vector.tensor_scalar(qk_bias[:, 0:1], col_sb[:, 0:1], float(HD) ** -0.5, None, ALU.mult)
                nc.vector.tensor_copy(qk_bias[:, 1:2], col_sb[:, 1:2]).then_inc(qk_bias_ready, 1)
                nc.vector.tensor_scalar(w_sb[:, FV, :], w_sb[:, FV, :], 0.5, None, ALU.mult).then_inc(fv_halved, 1)
                constant_rows()
                norm1_stats(1)
                norm_moments(0, 1, norm1_chain)
                for u in range(2):
                    dve.wait_ge(bias_loaded[u], 16)
                    for n in range(4 * GH):
                        maximum(u, 4 * u + n // NB, n % NB, n)

            def iteration(i, first=False, last=False):
                for g in range(GROUPS):
                    w = 4 * i + g
                    if first and g < 2:
                        dve.wait_ge(bias_loaded[g + 2], 16)
                    for s in range(STEPS):
                        at = STEPS * g + s
                        if has_norm1(i):
                            if at == DVE_AT["stats1"]:
                                norm1_stats(i + 2)
                            if at == DVE_AT["moments1"]:
                                norm_moments(0, i + 2, norm1_chain)
                        if at == DVE_AT["v"]:
                            if first:
                                dve.wait_ge(v_ones_ready, 1)
                            place_v(i)
                        if not first:
                            if at == DVE_AT["invert"]:
                                invert_sums(i - 1)
                            if at == DVE_AT["residual"]:
                                add_residual(i - 1)
                                norm2_stats(i - 1)
                            if at == DVE_AT["moments2"]:
                                norm_moments(1, i - 1, norm2_chain)
                            if at == DVE_AT["mix"]:
                                mix(i - 1)
                            if at == DVE_AT["gate"]:
                                gate_v(i - 1)
                        for n in (2 * s, 2 * s + 1):
                            if not last or g < 2:
                                maximum(w + 2, 4 * ((g + 2) % 4) + n // NB, n % NB, n)

            def epilogue():
                b = BATCH - 1
                invert_sums(b)
                norm_o(dve, nc.vector, b)
                add_residual(b)
                norm2_stats(b)
                norm_moments(1, b, norm2_chain)
                norm2(dve, nc.vector, b, BATCH)
                step_z(dve, nc.vector, b)
                mix(b)
                square_k(dve, nc.vector, b)
                gate_v(b)
                finish_y(dve, nc.vector, b)

            run(dve, prologue, iteration, epilogue)

        @block.gpsimd
        def _(pool):
            chain = [0]

            def link(ins):
                chain[0] += 1
                ins.then_inc(setup_pool, 1)
                pool.wait_ge(setup_pool, chain[0])

            def split_shift(u, n):
                wait(pool, shift_copied, u + 1)
                nc.gpsimd.tensor_tensor(shift_parts[n][:, 1, :], shift_f[:, :], shift_parts[n][:, 0, :],
                                        ALU.subtract).then_inc(shift_split, 1)

            def less_high(b, t):
                wait(pool, qk_copied, 2 * b + t + 1)
                nc.gpsimd.tensor_tensor(qk_f[:, t, :], qk_f[:, t, :], parts[:, t, 0, :],
                                        ALU.subtract).then_inc(qk_less_high, 1)

            def low_part(b, t):
                wait(pool, qk_mid_ready, 2 * b + t + 1)
                nc.gpsimd.tensor_tensor(parts[:, t, 2, :], qk_f[:, t, :], parts[:, t, 1, :],
                                        ALU.subtract).then_inc(qk_split, 1)

            def prologue():
                link(nc.gpsimd.memset(ident[:, :], 0.0))
                nc.gpsimd.affine_select(out=ident[:, :], in_=ident[:, :], compare_op=ALU.not_equal, fill=1.0,
                                        base=0, pattern=[[-1, P]], channel_multiplier=1).then_inc(ident_ready, 1)
                pool.wait_ge(ident_ready, 1)
                nc.gpsimd.tensor_copy(ident16[:, :], ident[:, :]).then_inc(ident_ready, 1)
                link(nc.gpsimd.memset(k_stack[:, :, :].bitcast(F32), 0.0))
                pool.sem_inc(stacks_zeroed, 1)
                pool.wait_ge(centre_ready, 1)
                for k, near, far in bucket_ranges(1 - P, BAND - 1):
                    a, b = BAND - 1 - far, BAND - near
                    ins = nc.gpsimd.tensor_copy(band_line[:, :, a:b],
                                                rb_parts[:, :, k:k + 1].to_broadcast([HEADS, 2, b - a]))
                ins.then_inc(band_line_ready, 1)
                less_high(0, 0)
                less_high(0, 1)
                low_part(0, 0)
                low_part(0, 1)
                pool.wait_ge(qk_split, 2)
                for r in range(3 * NB + 2):
                    a, b = (r % NB * P, (r % NB + 1) * P) if r < 3 * NB else (0, LEN)
                    rows = k_stack[CONST_ROW:P, 0, a:b]
                    link(nc.gpsimd.affine_select(out=rows, in_=rows, compare_op=ALU.not_equal, fill=1.0,
                                                 base=-r, pattern=[[0, b - a]], channel_multiplier=1))
                pool.sem_inc(k_const_built, 1)
                norm1(pool, nc.gpsimd, 1)
                nc.gpsimd.memset(v_sb[:, :, :, :], 1.0).then_inc(v_ones_ready, 1)
                nc.gpsimd.memset(z_t[:, 0:1], 0.0).then_inc(z_zero_ready, 1)
                split_shift(0, 0)
                pool.wait_ge(z_zero_ready, 1)
                pool.wait_ge(proj_bias_ready, 1)

            def iteration(i, first=False, last=False):
                for g in range(GROUPS):
                    w = 4 * i + g
                    for s in range(STEPS):
                        at = STEPS * g + s
                        if s == POOL_AT["shift"] and not (last and g == 3):
                            split_shift(w + 1, (g + 1) % 2)
                        if has_norm1(i) and at == POOL_AT["norm1"]:
                            norm1(pool, nc.gpsimd, i + 2)
                        if not last:
                            if at == POOL_AT["q_less"]:
                                less_high(i + 1, 0)
                            if at == POOL_AT["k_less"]:
                                less_high(i + 1, 1)
                            if at == POOL_AT["q_low"]:
                                low_part(i + 1, 0)
                            if at == POOL_AT["k_low"]:
                                low_part(i + 1, 1)
                        if not first:
                            if at == POOL_AT["norm_o"]:
                                norm_o(pool, nc.gpsimd, i - 1)
                            if at == POOL_AT["x_res"]:
                                bias_x_res(pool, nc.gpsimd, i - 1)
                            if at == POOL_AT["norm2"]:
                                norm2(pool, nc.gpsimd, i - 1, i + 1 if last else i + 2)
                            if at == POOL_AT["z_step"]:
                                step_z(pool, nc.gpsimd, i - 1)
                            if at == POOL_AT["square"]:
                                square_k(pool, nc.gpsimd, i - 1)
                            if at == POOL_AT["y"]:
                                finish_y(pool, nc.gpsimd, i - 1)

            def epilogue():
                bias_x_res(pool, nc.gpsimd, BATCH - 1)

            run(pool, prologue, iteration, epilogue)


def kernel(**inputs):
    import numpy as np
    import concourse.bacc as bacc
    from concourse.bass_utils import run_bass_kernel_spmd

    attn = {n: np.asarray(inputs[f"L0_attn_{n}"]) for n in ("x", "wq", "bq", "wk", "bk", "wv", "bv", "wo", "bo", "rel_bias")}
    ffn = {n: np.asarray(inputs[f"L0_ffn_{n}"]) for n in ("W_r", "W_k", "W_v", "mu_r", "mu_k")}
    arrays = {
        "x": attn["x"].reshape(BATCH, NB, P, DIM).transpose(0, 2, 1, 3),
        "weights": np.stack([w.T for w in (attn["wq"], attn["wk"], attn["wv"], attn["wo"],
                                           ffn["W_r"], ffn["W_k"], ffn["W_v"])], axis=1),
        "columns": np.stack([attn["bq"], attn["bk"], attn["bv"], ffn["mu_r"], ffn["mu_k"]], axis=1),
        "bo_row": attn["bo"].reshape(1, DIM),
        "rel_bias_t": attn["rel_bias"].T,
    }
    arrays = {n: np.ascontiguousarray(a) for n, a in arrays.items()}
    nc = bacc.Bacc("TRN2", target_bir_lowering=False, num_devices=1)
    args = [nc.dram_tensor(n, a.shape, mybir.dt.from_np(a.dtype), kind="ExternalInput").ap() for n, a in arrays.items()]
    y = nc.dram_tensor("y", (BATCH, P, NB, DIM), F32, kind="ExternalOutput").ap()
    attention_ffn_program(nc, *args, y)
    got = run_bass_kernel_spmd(nc, [arrays], core_ids=[0])
    return got.results[0]["y"].transpose(0, 2, 1, 3).reshape(BATCH, LEN, DIM)
```
